# Optimizing a Trainium2 kernel written in Bass

```python
import numpy as np
import jax
import jax.numpy as jnp

def _softmax(x, axis=-1):
    return jax.nn.softmax(x, axis=axis)

def _gelu(x):
    return jax.nn.gelu(x, approximate=True)

def _silu(x):
    return jax.nn.silu(x)

def _sigmoid(x):
    return jax.nn.sigmoid(x)

def _layernorm(x, axis=-1, eps=1e-05):
    m = jnp.mean(x, axis=axis, keepdims=True)
    v = jnp.var(x, axis=axis, keepdims=True)
    return (x - m) / jnp.sqrt(v + eps)

def _scatter_add(tgt, idx, src, axis=0):
    return tgt.at[idx].add(src)

def _segment_sum(src, seg, n):
    return jax.ops.segment_sum(src, seg, n)
kernel_name = 'mk_prb_d1_jaxref_r8_fe87ec'

def setup_inputs(seed: int=0):
    np.random.seed(seed)
    _w = jnp.asarray

    def _L0_attn_setup():
        import jax, jax.numpy as jnp
        import numpy as np
        B, L, D, H, W = (2, 128, 128, 16, 64)
        DH = D // H
        key = jax.random.key(seed)
        ks = jax.random.split(key, 7)
        scale = 0.02
        return {'x': jax.random.normal(ks[0], (B, L, D), dtype=jnp.float32), 'Wq': jax.random.normal(ks[1], (D, D), dtype=jnp.float32) * scale, 'Wk': jax.random.normal(ks[2], (D, D), dtype=jnp.float32) * scale, 'Wv': jax.random.normal(ks[3], (D, D), dtype=jnp.float32) * scale, 'Wo': jax.random.normal(ks[4], (D, D), dtype=jnp.float32) * scale, 'last_k_init': jax.random.normal(ks[5], (W - 1, H, DH), dtype=jnp.float32), 'last_v_init': jax.random.normal(ks[6], (W - 1, H, DH), dtype=jnp.float32)}
    _L0_attn_in = _L0_attn_setup()

    def _L0_ffn_setup():
        import jax, jax.numpy as jnp
        import numpy as np
        E = 32
        H = 128
        I = 64
        G = 8
        TKG = 4
        TOPK = 8
        NSH = 2
        SCALE = 2.5
        key = jax.random.key(seed)
        ks = jax.random.split(key, 10)
        s = 0.02
        return {'hidden_states': jax.random.normal(ks[0], (2, 128, H), jnp.float32), 'gate_w': jax.random.normal(ks[1], (E, H), jnp.float32) * s, 'gate_bias': jax.random.normal(ks[2], (E,), jnp.float32) * s, 'w_gate': jax.random.normal(ks[3], (E, I, H), jnp.float32) * s, 'w_up': jax.random.normal(ks[4], (E, I, H), jnp.float32) * s, 'w_down': jax.random.normal(ks[5], (E, H, I), jnp.float32) * s, 'sh_gate': jax.random.normal(ks[6], (I * NSH, H), jnp.float32) * s, 'sh_up': jax.random.normal(ks[7], (I * NSH, H), jnp.float32) * s, 'sh_down': jax.random.normal(ks[8], (H, I * NSH), jnp.float32) * s}
    _L0_ffn_in = _L0_ffn_setup()
    _d = {'L0_attn_x': _L0_attn_in['x'], 'L0_attn_Wq': _L0_attn_in['Wq'], 'L0_attn_Wk': _L0_attn_in['Wk'], 'L0_attn_Wv': _L0_attn_in['Wv'], 'L0_attn_Wo': _L0_attn_in['Wo'], 'L0_attn_last_k_init': _L0_attn_in['last_k_init'], 'L0_attn_last_v_init': _L0_attn_in['last_v_init'], 'L0_ffn_gate_w': _L0_ffn_in['gate_w'], 'L0_ffn_gate_bias': _L0_ffn_in['gate_bias'], 'L0_ffn_w_gate': _L0_ffn_in['w_gate'], 'L0_ffn_w_up': _L0_ffn_in['w_up'], 'L0_ffn_w_down': _L0_ffn_in['w_down'], 'L0_ffn_sh_gate': _L0_ffn_in['sh_gate'], 'L0_ffn_sh_up': _L0_ffn_in['sh_up'], 'L0_ffn_sh_down': _L0_ffn_in['sh_down']}
    _x0 = _d['L0_attn_x']
    _d['L0_attn_x'] = jax.random.normal(jax.random.fold_in(jax.random.key(seed), 1), (32, 256, 128), dtype=_x0.dtype)
    del _x0
    return _d

def reference(L0_attn_x, L0_attn_Wq, L0_attn_Wk, L0_attn_Wv, L0_attn_Wo, L0_attn_last_k_init, L0_attn_last_v_init, L0_ffn_gate_w, L0_ffn_gate_bias, L0_ffn_w_gate, L0_ffn_w_up, L0_ffn_w_down, L0_ffn_sh_gate, L0_ffn_sh_up, L0_ffn_sh_down):

    def _L0_attn_ref(x, Wq, Wk, Wv, Wo, last_k_init, last_v_init):
        import jax, jax.numpy as jnp
        import numpy as np
        B, L, D, H, W = (2, 128, 128, 16, 64)
        DH = D // H
        b, l, d = x.shape
        w1, h, dh = last_k_init.shape
        w = w1 + 1
        q = (x @ Wq.T).reshape(b, l, h, dh)
        k = (x @ Wk.T).reshape(b, l, h, dh)
        v = (x @ Wv.T).reshape(b, l, h, dh)
        last_k = jnp.broadcast_to(last_k_init[None], (b, w1, h, dh))
        last_v = jnp.broadcast_to(last_v_init[None], (b, w1, h, dh))
        k_pad = jnp.concatenate([last_k, k], axis=1)
        v_pad = jnp.concatenate([last_v, v], axis=1)
        idx = jnp.arange(l)[:, None] + jnp.arange(w)[None, :]
        k_win = k_pad[:, idx]
        v_win = v_pad[:, idx]
        scores = jnp.einsum('blhd,blwhd->blwh', q, k_win) * dh ** (-0.5)
        attn = jax.nn.softmax(scores, axis=2)
        out = jnp.einsum('blwh,blwhd->blhd', attn, v_win).reshape(b, l, d)
        return out @ Wo.T

    def _L0_ffn_ref(hidden_states, gate_w, gate_bias, w_gate, w_up, w_down, sh_gate, sh_up, sh_down):
        import jax, jax.numpy as jnp
        import numpy as np
        E = 32
        H = 128
        I = 64
        G = 8
        TKG = 4
        TOPK = 8
        NSH = 2
        SCALE = 2.5
        B, S, Hd = hidden_states.shape
        h = hidden_states.reshape(-1, Hd)
        logits = h.astype(jnp.float32) @ gate_w.T
        scores = jax.nn.sigmoid(logits)
        sc = scores + gate_bias
        grp = sc.reshape(-1, G, E // G)
        group_scores = jax.lax.top_k(grp, 2)[0].sum(-1)
        gidx = jax.lax.top_k(group_scores, TKG)[1]
        gmask = jnp.sum(jax.nn.one_hot(gidx, G, dtype=sc.dtype), axis=1)
        smask = jnp.repeat(gmask, E // G, axis=1)
        masked = jnp.where(smask > 0, sc, jnp.zeros_like(sc))
        tki = jax.lax.top_k(masked, TOPK)[1]
        tkw = jnp.take_along_axis(scores, tki, axis=1)
        tkw = tkw / (tkw.sum(-1, keepdims=True) + 1e-20)
        tkw = tkw * SCALE
        combine = (jax.nn.one_hot(tki, E, dtype=tkw.dtype) * tkw[..., None]).sum(1)
        g = jax.nn.silu(jnp.einsum('th,eih->tei', h, w_gate))
        u = jnp.einsum('th,eih->tei', h, w_up)
        routed = jnp.einsum('tei,ehi->th', g * u * combine[:, :, None], w_down)
        sg = jax.nn.silu(h @ sh_gate.T)
        shared = sg * (h @ sh_up.T) @ sh_down.T
        return (routed + shared).reshape(B, S, Hd)
    x = L0_attn_x
    xn = _layernorm(x, axis=-1)
    x = x + _L0_attn_ref(xn, L0_attn_Wq, L0_attn_Wk, L0_attn_Wv, L0_attn_Wo, L0_attn_last_k_init, L0_attn_last_v_init) + _L0_ffn_ref(xn, L0_ffn_gate_w, L0_ffn_gate_bias, L0_ffn_w_gate, L0_ffn_w_up, L0_ffn_w_down, L0_ffn_sh_gate, L0_ffn_sh_up, L0_ffn_sh_down)
    return x

_drawn_inputs = setup_inputs


def setup_inputs(seed=0):
    import zlib

    import numpy as np

    out = dict(_drawn_inputs(seed))
    spreads = {}
    factors = {'L0_attn_Wq': 8.0,
     'L0_attn_Wk': 8.0,
     'L0_attn_Wv': 8.0,
     'L0_attn_Wo': 4.646,
     'L0_attn_last_k_init': 8.0,
     'L0_attn_last_v_init': 5.649,
     'L0_ffn_gate_w': 8.0,
     'L0_ffn_gate_bias': 8.0,
     'L0_ffn_w_gate': 8.0,
     'L0_ffn_w_up': 8.0,
     'L0_ffn_w_down': 8.0,
     'L0_ffn_sh_gate': 8.0,
     'L0_ffn_sh_up': 8.0,
     'L0_ffn_sh_down': 8.0}
    for name, (base, spread) in spreads.items():
        noise = np.random.default_rng([zlib.crc32(name.encode()), seed]).standard_normal(out[name].shape)
        drawn = base * np.exp(spread * noise) if base else spread * noise
        out[name] = jnp.asarray(drawn.astype(out[name].dtype))
    for name, factor in factors.items():
        out[name] = (out[name] * factor).astype(out[name].dtype)
    return out
```

```python
from contextlib import ExitStack

import concourse.bass as bass
from concourse import mybir


def attention_and_experts(nc: bass.Bass, x, wq, wk, wv, wo, k_init, v_init, gate_w, gate_bias,
                          w_gate, w_up, w_down, sh_gate, sh_up, sh_down, out):
    f32, f32r, bf16 = mybir.dt.float32, mybir.dt.float32r, mybir.dt.bfloat16
    ALU, ACT, AX = mybir.AluOpType, mybir.ActivationFunctionType, mybir.AxisListType

    P = 128
    NSEQ, L, D = x.shape
    TB = 512
    NBLK = NSEQ * L // TB
    NT = TB // P
    SEQ = TB // L
    WIN = k_init.shape[0] + 1
    H, DH = k_init.shape[1:]
    HG = 4
    NG = H // HG
    NQ = L // WIN
    E, I, _ = w_gate.shape
    TOPK, NGRP, TKG, ROUTE_SCALE = 8, 8, 4, 2.5
    NJ = E * I // P + 1
    SH = NJ - 1
    SCALE = float(DH) ** -0.5
    NEG = -3.0e38
    TAKEN = -3.0e38
    Q_PART = [0, 1, 2, 0, 1, 0]
    K_PART = [0, 0, 0, 1, 1, 2]
    NR = len(Q_PART)
    M_ROW = NR * DH
    MASK_ROW = 64

    x_t = x.rearrange("(n s) (c p) d -> n p (s c) d", s=SEQ, p=P)
    out_t = out.rearrange("(n s) (c p) d -> n p (s c) d", s=SEQ, p=P)

    ctx = ExitStack()
    with ctx:
        def sb(name, shape, dt=f32):
            return ctx.enter_context(nc.sbuf_tensor(name, shape, dt))

        def sem(name):
            return ctx.enter_context(nc.semaphore(name))

        def dram(name, shape, dt):
            return nc.dram_tensor(name, shape, dt, kind="Internal").ap()

        q_dram = dram("q_dram", [P, 3, TB], bf16)
        k_dram = dram("k_dram", [P, 3, TB], bf16)
        ki_dram = dram("ki_dram", [P, 3, WIN], bf16)
        m_dram = dram("m_dram", [3 * H, TB], bf16)
        zero_dram = dram("zero_dram", [3, H * TB], bf16)
        den_dram = dram("den_dram", [NG, SEQ * NQ * HG * WIN], f32)
        rden_dram = dram("rden_dram", [NG, SEQ * NQ * HG * WIN], f32)

        ident = sb("ident", [P, P])
        identb = sb("identb", [P, P], bf16)
        onesf = sb("onesf", [P, 32])
        maskb = sb("maskb", [P, P], bf16)
        sel = sb("sel", [3 * E, SH, P], bf16)
        head_of_row = sb("head_of_row", [P, HG])
        bias = sb("bias", [P, E])
        half_neg = sb("half_neg", [P, NT])
        whi = sb("whi", [P, 2 * NJ + 2, P], f32r)
        wlo = sb("wlo", [P, 2 * NJ + 2, P], f32r)
        wf = sb("wf", [P, NJ + 3, P])
        wo_m = sb("wo_m", [P, HG, P])
        UP, WQ, WK = NJ, 2 * NJ, 2 * NJ + 1
        WV, WO, WR = NJ, NJ + 1, NJ + 2

        X = sb("X", [P, NT, P])
        XN = sb("XN", [P, NT, P])
        xnT = sb("xnT", [P, TB])
        xh_f = sb("xh_f", [P, TB], f32r)
        xl_f = sb("xl_f", [P, TB], f32r)
        stats = sb("stats", [P, NT, 6])
        mv = sb("mv", [P, NT, 2])
        veps = sb("veps", [P, NT])
        rstd = sb("rstd", [P, NT])
        QKF = sb("QKF", [P, 2, TB])
        QKR = sb("QKR", [P, 2, TB])
        QP = sb("QP", [P, 3, TB], bf16)
        KP = sb("KP", [P, 3, TB], bf16)
        V = sb("V", [P, SEQ, NQ, P])
        QS = sb("QS", [P, H, TB], bf16)
        KS = sb("KS", [P, 2, H, SEQ, 2 * P], bf16)
        NM = sb("NM", [P, NT, H])
        NMR = sb("NMR", [P, NT, H])
        NMP = sb("NMP", [P, NT, 3, H], bf16)
        MT = sb("MT", [3 * H, TB], bf16)
        ki = sb("ki", [P, WIN])
        kir = sb("kir", [P, WIN])
        kip = sb("kip", [P, 3, WIN], bf16)
        SC = sb("SC", [P, NT, E])
        SB_ = sb("SB_", [P, NT, E])
        pmax = sb("pmax", [P, NT * NGRP, 2])
        pmin = sb("pmin", [P, NT * NGRP, 2])
        g1 = sb("g1", [P, NT * NGRP])
        g2 = sb("g2", [P, NT * NGRP])
        g3 = sb("g3", [P, NT * NGRP])
        GS = sb("GS", [P, NT, NGRP + 4])
        GR = sb("GR", [P, NT, NGRP + 4])
        top = sb("top", [P, NT, 8])
        MS = sb("MS", [P, NT, E])
        MR = sb("MR", [P, NT, E])
        den4 = sb("den4", [P, NT])
        CW = sb("CW", [P, NT, E])
        CP = sb("CP", [P, NT, 3, E], bf16)
        CS = sb("CS", [3 * E, TB], bf16)
        xh = sb("xh", [P, TB], f32r)
        xl = sb("xl", [P, TB], f32r)
        TG = sb("TG", [P, 2, TB])
        H0 = sb("H0", [P, TB])
        H1 = sb("H1", [P, TB])
        HID = sb("HID", [P, 2, TB])
        PT = sb("PT", [P, 4, TB])
        PD = sb("PD", [P, SEQ * NQ, 2, HG * WIN])
        DC = sb("DC", [P, 64])
        RC = sb("RC", [P, 64])
        R = sb("R", [P, SEQ * NQ, HG, WIN])
        ON = sb("ON", [P, HG, SEQ * NQ, WIN])
        OT = sb("OT", [P, TB])
        XR = sb("XR", [P, NT, P])
        OS = sb("OS", [P, NT, P])

        def bank(name):
            return ctx.enter_context(nc.psum_tensor(name, [P, 512], f32))

        pG, pU, pC, pO, pS, pV = (bank(n) for n in ("pG", "pU", "pC", "pO", "pS", "pV"))
        pF = [bank("pF0"), bank("pF1")]

        stage = KS[:, :, :, :, :].rearrange("p a h s c -> p (a h s c)").bitcast(f32).rearrange("p (j c) -> p j c", c=P)
        J_G, J_U, J_Q = 0, NJ, 2 * NJ
        J_D = 2 * NJ + 2
        J_V, J_O, J_R, J_KI = J_D + NJ, J_D + NJ + 1, J_D + NJ + 2, J_D + NJ + 3
        NHL = J_D // 4
        NWT = J_KI // 4

        s_w = sem("weights_loaded")
        s_small = sem("small_loaded")
        s_const = sem("pool_constants")
        s_stage0 = sem("stage_cleared")
        s_wT = sem("weights_transposed")
        s_wc = sem("weights_copied")
        s_ki = sem("key_init_split")
        s_kid = sem("key_init_stored")
        s_kis = sem("key_init_stacked")
        s_zero = sem("zero_rows_stored")
        s_dset = sem("dve_setup_done")
        s_vinit = sem("value_init_loaded")
        s_vz = sem("value_row_zeroed")

        s_xl = sem("x_loaded")
        s_xn = sem("xn_done")
        s_var = sem("variance_done")
        s_rstd = sem("rstd_done")
        s_xT = sem("xT_copied")
        s_xhl = sem("xT_split")
        s_fr = sem("front_bank_ready")
        s_ff = [sem("front_bank0_free"), sem("front_bank1_free")]
        s_qkf = sem("qk_copied")
        s_p2 = sem("qk_parts12_done")
        s_p3 = sem("qk_part3_done")
        s_pst = sem("qk_parts_stored")
        s_stk = sem("stack_loaded")
        s_nm = sem("max_parts_done")
        s_mt = sem("max_rows_copied")
        s_md = sem("max_rows_stored")
        s_mr = sem("max_rows_stacked")
        s_ez = sem("router_exp_done")
        s_cp = sem("combine_parts_done")
        s_cs = sem("combine_rows_copied")
        s_xb = sem("x_handed_over")

        s_gr = sem("gate_ready")
        s_tg = sem("tanh_done")
        s_h0 = sem("gate_used")
        s_ur = sem("up_ready")
        s_h1 = sem("up_used")
        s_cr = sem("combine_bank_ready")
        s_hid = sem("hidden_ready")
        s_dn = sem("down_done")
        s_st = sem("scores_ready")
        s_ex = sem("exp_done")
        s_pv = sem("pv_done")
        s_pc = sem("pv_copied")
        s_dd = sem("den_stored")
        s_dc = sem("den_loaded")
        s_rc = sem("den_reciprocal")
        s_rd = sem("rden_stored")
        s_rl = sem("rden_loaded")
        s_on = sem("attention_normalised")
        s_or = sem("outT_ready")
        s_oc = sem("outT_copied")
        s_fT = sem("out_transposed")
        s_fa = sem("residual_added")
        s_xr = sem("residual_loaded")
        s_os = sem("out_stored")
        s_dve = sem("dve_chain")
        s_passed, s_passed_pe, s_passed_dve = (sem(f"waits_passed_{e}") for e in ("sp", "pe", "dve"))

        NFU = 24
        NS = SEQ * NQ * 2
        NSTK = NR * (2 + SEQ) + 1
        block = ctx.enter_context(nc.Block())

        @block.sync
        def _(sp):
            def rows(ap):
                return ap.rearrange("(j p) d -> p j d", p=P)

            sp.dma_start(X[:, :, :], x_t[0]).then_inc(s_xl, 16)
            sp.wait_ge(s_stage0, 1)
            sp.dma_start(stage[:, J_Q, :], wq).then_inc(s_w, 16)
            sp.dma_start(stage[:, J_Q + 1, :], wk).then_inc(s_w, 16)
            sp.dma_start(stage[:, J_V, :], wv).then_inc(s_w, 16)
            sp.dma_start(stage[:, J_O, :], wo).then_inc(s_w, 16)
            sp.dma_start(stage[0:E, J_R, :], gate_w).then_inc(s_w, 16)
            sp.dma_start(stage[1:WIN, J_KI, :], k_init.rearrange("w h d -> w (h d)")).then_inc(s_w, 16)
            sp.dma_start(stage[:, J_G:J_G + SH, :], rows(w_gate.rearrange("e i h -> (e i) h"))).then_inc(s_w, 16)
            sp.dma_start(stage[:, J_G + SH, :], sh_gate).then_inc(s_w, 16)
            sp.dma_start(stage[:, J_U:J_U + SH, :], rows(w_up.rearrange("e i h -> (e i) h"))).then_inc(s_w, 16)
            sp.dma_start(stage[:, J_U + SH, :], sh_up).then_inc(s_w, 16)
            sp.dma_start(stage[:, J_D:J_D + SH, :].rearrange("p j (a i) -> p (j a) i", i=I),
                         w_down.rearrange("e h i -> h e i")).then_inc(s_w, 16)
            sp.dma_start(stage[:, J_D + SH, :], sh_down).then_inc(s_w, 16)
            sp.dma_start(bias[:, :], gate_bias.rearrange("(a e) -> a e", a=1).broadcast_to([P, E])).then_inc(s_small, 16)
            sp.wait_ge(s_vz, 1)
            for s in range(SEQ):
                sp.dma_start(V[1:WIN, s, 0, :], v_init.rearrange("w h d -> w (h d)")).then_inc(s_vinit, 16)
            sp.wait_ge(s_ki, 1)
            sp.dma_start(ki_dram, kip[:, :, :]).then_inc(s_kid, 16)
            sp.dma_start(zero_dram, QS[32:35, :, :]).then_inc(s_zero, 16)
            sp.wait_ge(s_kid, 16)
            sp.wait_ge(s_zero, 16)
            for r in range(NR):
                src = ki_dram[:, K_PART[r], :].rearrange("(h d) w -> d h w", d=DH)
                for s in range(SEQ):
                    sp.dma_start(KS[DH * r:DH * r + DH, 0, :, s, 0:WIN], src).then_inc(s_kis, 16)

            def wait(sem, value):
                sp.wait_ge(sem, value)
                if not isinstance(value, int):
                    sp.sem_inc(s_passed, 1)

            def front_loads(m):
                if not isinstance(m, int) or m > 0:
                    wait(s_stk, m * (16 * NSTK))
                wait(s_p3, 2 * m + 1)
                wait(s_p2, 2 * m + 1)
                sp.dma_start(q_dram, QP[:, :, :]).then_inc(s_pst, 16)
                wait(s_p3, 2 * m + 2)
                wait(s_p2, 2 * m + 2)
                sp.dma_start(k_dram, KP[:, :, :]).then_inc(s_pst, 16)
                wait(s_pst, 32 * m + 32)
                wait(s_st, NS * m)
                sp.dma_start(QS[M_ROW:M_ROW + 3, :, :].rearrange("p h t -> p (h t)"), zero_dram).then_inc(s_stk, 16)
                for r in range(NR):
                    sp.dma_start(QS[DH * r:DH * r + DH, :, :],
                                 q_dram[:, Q_PART[r], :].rearrange("(h d) t -> d h t", d=DH)).then_inc(s_stk, 16)
                    rows_r = slice(DH * r, DH * r + DH)
                    src = k_dram[:, K_PART[r], :].rearrange("(h d) t -> d h t", d=DH)
                    sp.dma_start(KS[rows_r, 1, :, :, :].rearrange("p h s t -> p h (s t)"), src).then_inc(s_stk, 16)
                    for s in range(SEQ):
                        sp.dma_start(KS[rows_r, 0, :, s, WIN:L], src[:, :, s * L:(s + 1) * L - WIN]).then_inc(s_stk, 16)

            def max_rows(m):
                wait(s_mt, m + 1)
                sp.dma_start(m_dram, MT[:, :]).then_inc(s_md, 16)
                wait(s_md, 16 * m + 16)
                sp.dma_start(QS[M_ROW:M_ROW + 3, :, :],
                             m_dram.rearrange("(a h) t -> a h t", a=3)).then_inc(s_mr, 16)

            def denominators(n):
                wait(s_pc, SEQ * NQ * (n + 1))
                sp.dma_start(den_dram.rearrange("g (u c) -> g u c", c=HG * WIN), PD[0:97:32, :, 1, :]).then_inc(s_dd, 16)
                wait(s_dd, 16 * n + 16)
                sp.dma_start(DC[:, :], den_dram.rearrange("g (a c) -> (g a) c", c=64)).then_inc(s_dc, 16)
                wait(s_rc, n + 1)
                sp.dma_start(rden_dram.rearrange("g (a c) -> (g a) c", c=64), RC[:, :]).then_inc(s_rd, 16)
                wait(s_rd, 16 * n + 16)
                wait(s_on, n)
                for g in range(NG):
                    sp.dma_start(R[32 * g:32 * g + 32, :, :, :].rearrange("p u h q -> p (u h q)"),
                                 rden_dram[g:g + 1, :].broadcast_to([32, SEQ * NQ * HG * WIN])).then_inc(s_rl, 16)

            def store(n):
                wait(s_fa, n + 1)
                sp.dma_start(out_t[n], OS[:, :, :]).then_inc(s_os, 16)

            def iteration(n, ahead):
                wait(s_fa, n)
                sp.dma_start(XR[:, :, :], x_t[n]).then_inc(s_xr, 16)
                if ahead:
                    wait(s_xn, n + 1)
                    sp.dma_start(X[:, :, :], x_t[n + 1]).then_inc(s_xl, 16)
                    front_loads(n + 1)
                denominators(n)
                if ahead:
                    max_rows(n + 1)
                store(n)

            front_loads(0)
            max_rows(0)
            iteration(0, True)
            with sp.Fori(1, NBLK - 1) as n:
                iteration(n, True)
            iteration(NBLK - 1, False)
            sp.wait_ge(s_os, 16 * NBLK)

        @block.gpsimd
        def _(pool):
            pool.memset(ident[:, :], 0.0).then_inc(s_const, 1)
            pool.memset(maskb[:, :], 0.0).then_inc(s_const, 1)
            pool.memset(sel[:, :, :], 0.0).then_inc(s_const, 1)
            pool.memset(onesf[:, :], 1.0).then_inc(s_const, 1)
            pool.memset(half_neg[:, :], -0.5).then_inc(s_const, 1)
            pool.wait_ge(s_const, 5)
            pool.affine_select(out=ident[:, :], in_=ident[:, :], compare_op=ALU.not_equal, fill=1.0,
                               base=0, pattern=[[-1, P]], channel_multiplier=1).then_inc(s_const, 1)
            pool.affine_select(out=maskb[:, :], in_=maskb[:, :], compare_op=ALU.is_ge, fill=NEG,
                               base=WIN - 1, pattern=[[1, P]], channel_multiplier=-1).then_inc(s_const, 1)
            pool.wait_ge(s_const, 7)
            pool.affine_select(out=maskb[:, :], in_=maskb[:, :], compare_op=ALU.is_ge, fill=NEG,
                               base=0, pattern=[[-1, P]], channel_multiplier=1).then_inc(s_const, 1)
            for a in range(3):
                pool.wait_ge(s_const, 8 + a)
                part = sel[:, :, :].rearrange("p j (b i) -> p j b i", b=2)
                pool.affine_select(out=part, in_=part, compare_op=ALU.not_equal, fill=1.0, base=-E * a,
                                   pattern=[[-2, SH], [-1, 2], [0, I]], channel_multiplier=1).then_inc(s_const, 1)

            def front(m):
                pool.wait_ge(s_var, m + 1)
                pool.tensor_tensor(rstd[:, :], veps[:, :], half_neg[:, :], ALU.pow).then_inc(s_rstd, 1)
                for i, parts in enumerate((QP, KP)):
                    pool.wait_ge(s_p2, 2 * m + i + 1)
                    pool.tensor_tensor(parts[:, 2, :], QKR[:, i, :], parts[:, 1, :], ALU.subtract).then_inc(s_p3, 1)

            def back(n):
                pool.wait_ge(s_rl, 16 * NG * (n + 1))
                pool.wait_ge(s_or, n)
                pool.tensor_tensor(ON[:, :, :, :],
                                   PD[:, :, 0, :].rearrange("p u (h q) -> p h u q", h=HG),
                                   R[:, :, :, :].rearrange("p u h q -> p h u q"), ALU.mult).then_inc(s_on, 1)

            front(0)
            front(1)
            back(0)
            with pool.Fori(1, NBLK - 1) as n:
                front(n + 1)
                back(n)
            back(NBLK - 1)

        @block.tensor
        def _(pe):
            def split3(dst, w, hi, lo):
                nc.tensor.matmul(dst, whi[:, w, :], hi, start=True, stop=False)
                nc.tensor.matmul(dst, whi[:, w, :], lo, start=False, stop=False)
                return nc.tensor.matmul(dst, wlo[:, w, :], hi, start=False, stop=True)

            pe.wait_ge(s_const, 11)
            pe.wait_ge(s_w, 16 * 12)
            for k in range(NWT + 1):
                if k >= 2:
                    pe.wait_ge(s_wc, k - 1)
                for i in range(4 if k < NWT else 1):
                    last = nc.tensor.transpose(pF[k % 2][:, i * P:(i + 1) * P], stage[:, 4 * k + i, :], ident[:, :])
                last.then_inc(s_wT, 1)
            pe.wait_ge(s_wc, NWT + 1)

            def use(m, u):
                pe.wait_ge(s_ff[u % 2], m * (NFU // 2) + u // 2)
                return pF[u % 2]

            def front_x(m):
                b = use(m, 0)
                pe.wait_ge(s_xn, m + 1)
                for t in range(NT):
                    last = nc.tensor.transpose(b[:, t * P:(t + 1) * P], XN[:, t, :], ident[:, :])
                last.then_inc(s_fr, 1)

            def front_qk(m):
                pe.wait_ge(s_xhl, m + 1)
                for i, w in enumerate((WQ, WK)):
                    b = use(m, 1 + i)
                    split3(b[:, :], w, xh_f[:, :], xl_f[:, :]).then_inc(s_fr, 1)

            def front_v(m, s):
                b = use(m, 3 + s)
                t0 = s * L
                nc.tensor.matmul(b[WIN:P, 0:P], xnT[:, t0:t0 + WIN], wf[:, WV, :], start=True, stop=True)
                for w in range(1, NQ):
                    t = t0 + (w - 1) * WIN
                    last = nc.tensor.matmul(b[:, w * P:(w + 1) * P], xnT[:, t:t + P], wf[:, WV, :],
                                            start=True, stop=True)
                last.then_inc(s_fr, 1)

            def front_router(m):
                b = use(m, 5)
                for t in range(NT):
                    last = nc.tensor.matmul(b[:, t * E:(t + 1) * E], xnT[:, t * P:(t + 1) * P],
                                            wf[:, WR, 0:E], start=True, stop=True)
                last.then_inc(s_fr, 1)

            def front_scores(m, k):
                b = use(m, 6 + k)
                t, hg = divmod(k, NG)
                s, c = divmod(t, L // P)
                if k == 0:
                    pe.wait_ge(s_stk, (m + 1) * (16 * NSTK))
                for i in range(HG):
                    h = hg * HG + i
                    for half in range(2):
                        q0 = t * P + half * WIN
                        last = nc.tensor.matmul(b[half * WIN:(half + 1) * WIN, i * P:(i + 1) * P],
                                                QS[:, h, q0:q0 + WIN], KS[:, half, h, s, c * P:(c + 1) * P],
                                                start=True, stop=True)
                last.then_inc(s_fr, 1)

            def front_max(m):
                b = use(m, 22)
                pe.wait_ge(s_nm, m + 1)
                pe.sem_inc(s_passed_pe, 1)
                bb = b[:, :].bitcast(bf16)
                for t in range(NT):
                    last = nc.tensor.transpose(bb[0:3 * H, t * P:(t + 1) * P],
                                               NMP[:, t, :, :].rearrange("p a h -> p (a h)"), identb[:, :])
                last.then_inc(s_fr, 1)

            def front_combine(m):
                b = use(m, 23)
                pe.wait_ge(s_cp, m + 1)
                bb = b[:, :].bitcast(bf16)
                for t in range(NT):
                    last = nc.tensor.transpose(bb[0:3 * E, t * P:(t + 1) * P],
                                               CP[:, t, :, :].rearrange("p a e -> p (a e)"), identb[:, :])
                last.then_inc(s_fr, 1)

            def gate_up(n, j):
                if j == 0:
                    pe.wait_ge(s_xb, n + 1)
                pe.wait_ge(s_h0, NJ * n + j)
                split3(pG[:, :], j, xh[:, :], xl[:, :]).then_inc(s_gr, 1)
                pe.wait_ge(s_h1, NJ * n + j)
                split3(pU[:, :], UP + j, xh[:, :], xl[:, :]).then_inc(s_ur, 1)
                if j < SH:
                    if j == 0:
                        pe.wait_ge(s_cs, n + 1)
                    pe.wait_ge(s_hid, NJ * n + j)
                    nc.tensor.matmul(pC[:, :], sel[:, j, :], CS[:, :], start=True, stop=True).then_inc(s_cr, 1)

            def down(n, j):
                if j == 0:
                    pe.wait_ge(s_oc, n)
                pe.wait_ge(s_hid, NJ * n + j + 1)
                nc.tensor.matmul(pO[:, :], wf[:, j, :], HID[:, j % 2, :], start=j == 0, stop=False).then_inc(s_dn, 1)

            def scores(n, k):
                u, half = divmod(k, 2)
                s, w = divmod(u, NQ)
                if k == 0:
                    pe.wait_ge(s_mr, 16 * n + 16)
                    pe.wait_ge(s_fa, n)
                pe.wait_ge(s_ex, NS * n + k)
                q0 = s * L + w * WIN
                for i in range(8):
                    h = half * 8 + i
                    last = nc.tensor.matmul(pS[:, i * WIN:(i + 1) * WIN],
                                            KS[:, w % 2, h, s, (w // 2) * P:(w // 2 + 1) * P],
                                            QS[:, h, q0:q0 + WIN], start=True, stop=True)
                last.then_inc(s_st, 1)

            def weigh(n, k):
                u, half = divmod(k, 2)
                s, w = divmod(u, NQ)
                if half == 0:
                    pe.wait_ge(s_pc, SEQ * NQ * n + u)
                pe.wait_ge(s_ex, NS * n + k + 1)
                W4 = HG * WIN
                for i in range(2):
                    g = 2 * half + i
                    p = PT[:, k % 4, i * W4:(i + 1) * W4]
                    nc.tensor.matmul(pV[32 * g:32 * g + 32, 0:W4], V[:, s, w, 32 * g:32 * g + 32], p,
                                     start=True, stop=True)
                    last = nc.tensor.matmul(pV[32 * g:32 * g + 32, W4:2 * W4], onesf[:, :], p,
                                            start=True, stop=True)
                last.then_inc(s_pv, 1)

            def project_out(n):
                pe.wait_ge(s_on, n + 1)
                for i in range(HG):
                    last = nc.tensor.matmul(pO[:, :], wo_m[:, i, :], ON[:, i, :, :].rearrange("p u q -> p (u q)"),
                                            start=False, stop=i == HG - 1)
                last.then_inc(s_or, 1)

            def finish(n):
                pe.wait_ge(s_oc, n + 1)
                pe.wait_ge(s_ex, NS * (n + 1))
                for t in range(NT):
                    last = nc.tensor.transpose(pS[:, t * P:(t + 1) * P], OT[:, t * P:(t + 1) * P], ident[:, :])
                last.then_inc(s_fT, 1)

            def iteration(n, ahead):
                m = n + 1
                for j in range(NJ):
                    gate_up(n, j)
                    if j >= 2:
                        down(n, j - 2)
                    if 1 <= j <= 6:
                        for k in range((j - 1) * 3, min(NS, j * 3)):
                            scores(n, k)
                            if k >= 1:
                                weigh(n, k - 1)
                    if j == 7:
                        weigh(n, NS - 1)
                    if ahead:
                        if j == 1:
                            front_x(m)
                        elif j == 2:
                            front_qk(m)
                        elif j == 7:
                            front_v(m, 0)
                        elif j == 8:
                            front_v(m, 1)
                            front_router(m)
                        elif j >= 9:
                            for k in range((j - 9) * 2, (j - 9) * 2 + 2):
                                front_scores(m, k)
                down(n, NJ - 2)
                if ahead:
                    front_max(m)
                down(n, NJ - 1)
                if ahead:
                    front_combine(m)
                project_out(n)
                finish(n)

            front_x(0)
            front_qk(0)
            for s in range(SEQ):
                front_v(0, s)
            front_router(0)
            pe.wait_ge(s_dset, 6)
            pe.wait_ge(s_kis, 16 * NR * SEQ)
            pe.wait_ge(s_vinit, 16 * SEQ)
            for k in range(NT * NG):
                front_scores(0, k)
            front_max(0)
            front_combine(0)
            iteration(0, True)
            with pe.Fori(1, NBLK - 1) as n:
                iteration(n, True)
            iteration(NBLK - 1, False)

        @block.scalar
        def _(act):
            copy = ACT.Copy
            for k in range(NHL, NWT + 1):
                act.wait_ge(s_wT, k + 1)
                if k < NWT:
                    act.wait_ge(s_wc, k)
                    nc.scalar.activation(wf[:, 4 * (k - NHL):4 * (k - NHL) + 4, :].rearrange("p j c -> p (j c)"),
                                         pF[k % 2][:, :], copy).then_inc(s_wc, 1)
                else:
                    act.wait_ge(s_wc, k)
                    nc.scalar.activation(ki[:, :], pF[k % 2][:, 0:WIN], copy).then_inc(s_wc, 1)

            def copied(u):
                return s_ff[u % 2]

            def front_x(m):
                act.wait_ge(s_fr, NFU * m + 1)
                nc.scalar.activation(xnT[:, :], pF[0][:, :], copy).then_inc(s_xT, 1)
                act.wait_ge(s_xT, m + 1)
                act.sem_inc(copied(0), 1)

            def front_qk(m):
                for i in range(2):
                    act.wait_ge(s_fr, NFU * m + 2 + i)
                    act.wait_ge(s_p3, 2 * m + i)
                    nc.scalar.activation(QKF[:, i, :], pF[(1 + i) % 2][:, :], copy,
                                         scale=SCALE if i == 0 else 1.0).then_inc(s_qkf, 1)
                    act.wait_ge(s_qkf, 2 * m + i + 1)
                    act.sem_inc(copied(1 + i), 1)

            def front_v(m):
                act.wait_ge(s_pv, NS * m)
                for s in range(SEQ):
                    act.wait_ge(s_fr, NFU * m + 4 + s)
                    b = pF[(3 + s) % 2]
                    nc.scalar.activation(V[WIN:P, s, 0, :], b[WIN:P, 0:P], copy)
                    nc.scalar.activation(V[:, s, 1:NQ, :].rearrange("p w c -> p (w c)"), b[:, P:NQ * P],
                                         copy).then_inc(copied(3 + s), 1)

            def front_router(m):
                act.wait_ge(s_fr, NFU * m + 6)
                nc.scalar.activation(SC[:, :, :].rearrange("p t e -> p (t e)"), pF[5 % 2][:, 0:NT * E],
                                     ACT.Exp, scale=-1.0).then_inc(s_ez, 1)
                act.wait_ge(s_ez, m + 1)
                act.sem_inc(copied(5), 1)

            def front_rows(m):
                act.wait_ge(s_fr, NFU * m + 23)
                act.wait_ge(s_md, 16 * m)
                nc.scalar.activation(MT[:, :], pF[22 % 2][0:3 * H, :].bitcast(bf16)[:, 0:TB], copy).then_inc(s_mt, 1)
                act.wait_ge(s_mt, m + 1)
                act.sem_inc(copied(22), 1)
                act.wait_ge(s_fr, NFU * m + 24)
                act.wait_ge(s_cr, SH * m)
                nc.scalar.activation(CS[:, :], pF[23 % 2][0:3 * E, :].bitcast(bf16)[:, 0:TB], copy).then_inc(s_cs, 1)
                act.wait_ge(s_cs, m + 1)
                act.sem_inc(copied(23), 1)

            def gate(n, j):
                act.wait_ge(s_gr, NJ * n + j + 1)
                act.wait_ge(s_h0, NJ * n + max(j - 1, 0))
                nc.scalar.activation(TG[:, j % 2, :], pG[:, :], ACT.Tanh, scale=0.5).then_inc(s_tg, 1)

            def exps(n, k):
                act.wait_ge(s_st, NS * n + k + 1)
                act.wait_ge(s_pv, NS * n + max(k - 3, 0))
                nc.scalar.activation(PT[:, k % 4, :], pS[:, :], ACT.Exp).then_inc(s_ex, 1)

            def copy_pv(n, u):
                act.wait_ge(s_pv, NS * n + 2 * u + 2)
                if u == 0:
                    act.wait_ge(s_on, n)
                    act.wait_ge(s_dd, 16 * n)
                nc.scalar.activation(PD[:, u, :, :].rearrange("p a c -> p (a c)"), pV[:, :], copy).then_inc(s_pc, 1)

            def iteration(n, ahead):
                m = n + 1
                for j in range(NJ):
                    gate(n, j)
                    if 1 <= j <= 6:
                        for k in range((j - 1) * 3, min(NS, j * 3)):
                            exps(n, k)
                            if k >= 2 and k % 2 == 0:
                                copy_pv(n, k // 2 - 1)
                    if j == 7:
                        copy_pv(n, NS // 2 - 1)
                    if ahead:
                        if j == 1:
                            front_x(m)
                        elif j == 2:
                            front_qk(m)
                        elif j == 8:
                            front_v(m)
                            front_router(m)
                if ahead:
                    front_rows(m)
                act.wait_ge(s_or, n + 1)
                act.wait_ge(s_fT, n)
                nc.scalar.activation(OT[:, :], pO[:, :], copy).then_inc(s_oc, 1)

            front_x(0)
            front_qk(0)
            front_v(0)
            front_router(0)
            front_rows(0)
            iteration(0, True)
            with act.Fori(1, NBLK - 1) as n:
                iteration(n, True)
            iteration(NBLK - 1, False)

        @block.vector
        def _(dve):
            v = nc.vector
            chain = {"base": 0, "k": 0}

            def link_apart(ins):
                chain["k"] += 1
                ins.then_inc(s_dve, 1)
                dve.wait_ge(s_dve, chain["base"] + chain["k"])
                dve.sem_inc(s_passed_dve, 1)

            def link(ins):
                chain["k"] += 1
                ins.then_inc(s_dve, 1)
                dve.wait_ge(s_dve, chain["base"] + chain["k"])

            v.memset(stage[:, J_R:J_KI + 1, :], 0.0).then_inc(s_stage0, 1)
            v.memset(QS[0:MASK_ROW, :, :], 0.0).then_inc(s_dset, 1)
            for s in range(SEQ):
                last = v.memset(V[0:32, s, 0, :], 0.0)
            last.then_inc(s_vz, 1)
            v.memset(GS[:, :, NGRP:NGRP + 4], 3.0e38).then_inc(s_dset, 1)
            dve.wait_ge(s_const, 11)
            link(v.tensor_copy(identb[:, :], ident[:, :]))
            for k in range(NHL):
                dve.wait_ge(s_wT, k + 1)
                hi = whi[:, 4 * k:4 * k + 4, :].rearrange("p j c -> p (j c)")
                lo = wlo[:, 4 * k:4 * k + 4, :].rearrange("p j c -> p (j c)")
                link(v.tensor_copy(hi, pF[k % 2][:, :]))
                v.tensor_tensor(lo, pF[k % 2][:, :], hi.bitcast(f32), ALU.subtract).then_inc(s_wc, 1)
            dve.wait_ge(s_wc, NWT + 1)
            link(v.tensor_copy(kip[:, 0, :], ki[:, :]))
            link(v.tensor_tensor(kir[:, :], ki[:, :], kip[:, 0, :], ALU.subtract))
            link(v.tensor_copy(kip[:, 1, :], kir[:, :]))
            v.memset(KS[32:MASK_ROW, :, :, :, :].rearrange("p a h s c -> p (a h s c)"), 1.0).then_inc(s_dset, 1)
            v.memset(KS[0:32, :, :, :, :].rearrange("p a h s c -> p (a h s c)").bitcast(f32), 0.0).then_inc(s_dset, 1)
            dve.wait_ge(s_dset, 4)
            v.tensor_tensor(kip[:, 2, :], kir[:, :], kip[:, 1, :], ALU.subtract).then_inc(s_ki, 1)
            v.tensor_copy(KS[MASK_ROW:P, :, :, :, :].rearrange("p a h s (c r) -> p (a h s c) r", r=P),
                          maskb[MASK_ROW:P, :].rearrange("p (a r) -> p a r", a=1)
                          .broadcast_to([P - MASK_ROW, 2 * H * SEQ * 2, P])).then_inc(s_dset, 1)
            v.tensor_copy(QS[MASK_ROW:P, :, :].rearrange("p h (c q) -> p (h c) q", q=WIN),
                          identb[MASK_ROW:P, MASK_ROW:P].rearrange("p (a q) -> p a q", a=1)
                          .broadcast_to([WIN, H * NT * 2, WIN])).then_inc(s_dset, 1)
            link(v.tensor_reduce(head_of_row[:, :], ident[:, :].rearrange("p (g h d) -> p h g d", g=NG, h=HG),
                                 AX.XY, ALU.add))
            for i in range(HG):
                last = v.tensor_scalar(wo_m[:, i, :], wf[:, WO, :], head_of_row[:, i:i + 1], None, ALU.mult)
            link(last)
            dve.wait_ge(s_small, 16)

            def front_norm(m):
                dve.wait_ge(s_xl, 16 * m + 16)
                for t in range(NT):
                    last = v.bn_stats(stats[:, t, :], X[:, t, :])
                link_apart(last)
                for t in range(NT):
                    last = v.bn_aggr(mv[:, t, :], stats[:, t, :])
                link(last)
                v.tensor_scalar(veps[:, :], mv[:, :, 1], 1e-5, None, ALU.add).then_inc(s_var, 1)
                dve.wait_ge(s_rstd, m + 1)
                dve.wait_ge(s_fr, NFU * m)
                for t in range(NT):
                    last = v.tensor_scalar(XN[:, t, :], X[:, t, :], mv[:, t, 0:1], rstd[:, t:t + 1],
                                           ALU.subtract, ALU.mult)
                last.then_inc(s_xn, 1)

            def front_split(m):
                dve.wait_ge(s_xT, m + 1)
                link(v.tensor_copy(xh_f[:, :], xnT[:, :]))
                v.tensor_tensor(xl_f[:, :], xnT[:, :], xh_f[:, :].bitcast(f32), ALU.subtract).then_inc(s_xhl, 1)

            def front_qk(m, i):
                parts = (QP, KP)[i]
                dve.wait_ge(s_qkf, 2 * m + i + 1)
                dve.wait_ge(s_pst, 32 * m)
                link(v.tensor_copy(parts[:, 0, :], QKF[:, i, :]))
                link(v.tensor_tensor(QKR[:, i, :], QKF[:, i, :], parts[:, 0, :], ALU.subtract))
                v.tensor_copy(parts[:, 1, :], QKR[:, i, :]).then_inc(s_p2, 1)

            def flat(t):
                return t[:, :, :].rearrange("p t e -> p (t e)")

            def front_route_a(m):
                dve.wait_ge(s_ez, m + 1)
                link(v.tensor_scalar(flat(MR), flat(SC), 1.0, None, ALU.add))
                link(v.reciprocal(flat(SC), flat(MR)))
                link(v.tensor_tensor(SB_[:, :, :], SC[:, :, :],
                                     bias[:, :].rearrange("p (a e) -> p a e", a=1).broadcast_to([P, NT, E]), ALU.add))
                pairs = flat(SB_).rearrange("p (g a b) -> p g a b", a=2, b=2)
                v.tensor_tensor(pmax[:, :, :], pairs[:, :, :, 0], pairs[:, :, :, 1], ALU.max)
                link(v.tensor_tensor(pmin[:, :, :], pairs[:, :, :, 0], pairs[:, :, :, 1], ALU.min))
                v.tensor_tensor(g1[:, :], pmax[:, :, 0], pmax[:, :, 1], ALU.max)
                v.tensor_tensor(g2[:, :], pmax[:, :, 0], pmax[:, :, 1], ALU.min)
                link(v.tensor_tensor(g3[:, :], pmin[:, :, 0], pmin[:, :, 1], ALU.max))
                link(v.tensor_tensor(g2[:, :], g2[:, :], g3[:, :], ALU.max))
                link(v.tensor_tensor(GS[:, :, 0:NGRP], g1[:, :].rearrange("p (t g) -> p t g", t=NT),
                                     g2[:, :].rearrange("p (t g) -> p t g", t=NT), ALU.add))

            def front_route_b(m):
                for t in range(NT):
                    last = v.max(top[:, t, :], GS[:, t, :])
                link_apart(last)
                for t in range(NT):
                    last = v.match_replace(out=GR[:, t, :], in_to_replace=top[:, t, :], in_values=GS[:, t, :],
                                           imm_value=TAKEN)
                link(last)
                link(v.tensor_scalar(GR[:, :, 0:NGRP], GR[:, :, 0:NGRP], TAKEN, None, ALU.is_equal))
                link(v.tensor_tensor(MS[:, :, :].rearrange("p t (g a) -> p t g a", g=NGRP),
                                     SB_[:, :, :].rearrange("p t (g a) -> p t g a", g=NGRP),
                                     GR[:, :, 0:NGRP].rearrange("p t (g a) -> p t g a", a=1)
                                     .broadcast_to([P, NT, NGRP, E // NGRP]), ALU.mult))
                link(v.tensor_scalar(flat(MS), flat(MS), 0.0, None, ALU.add))

            def front_route_c(m):
                for t in range(NT):
                    last = v.max(top[:, t, :], MS[:, t, :])
                link_apart(last)
                for t in range(NT):
                    last = v.match_replace(out=MR[:, t, :], in_to_replace=top[:, t, :], in_values=MS[:, t, :],
                                           imm_value=TAKEN)
                link(last)
                link(v.scalar_tensor_tensor(out=flat(CW), in0=flat(MR), scalar=TAKEN, in1=flat(SC),
                                            op0=ALU.is_equal, op1=ALU.mult))
                link(v.tensor_reduce(den4[:, :], CW[:, :, :], AX.X, ALU.add))
                link(v.tensor_scalar(den4[:, :], den4[:, :], 1e-20, None, ALU.add))
                link(v.reciprocal(den4[:, :], den4[:, :]))
                for t in range(NT):
                    last = v.tensor_scalar(CW[:, t, :], CW[:, t, :], den4[:, t:t + 1], ROUTE_SCALE, ALU.mult, ALU.mult)
                link(last)
                link(v.tensor_copy(CP[:, :, 0, :], CW[:, :, :]))
                link(v.tensor_tensor(CW[:, :, :], CW[:, :, :], CP[:, :, 0, :], ALU.subtract))
                link(v.tensor_copy(CP[:, :, 1, :], CW[:, :, :]))
                v.tensor_tensor(CP[:, :, 2, :], CW[:, :, :], CP[:, :, 1, :], ALU.subtract).then_inc(s_cp, 1)

            def front_max(m, k):
                t, hg = divmod(k, NG)
                dve.wait_ge(s_fr, NFU * m + 7 + k)
                v.tensor_reduce(NM[:, t, hg * HG:(hg + 1) * HG],
                                pF[(6 + k) % 2][:, :].rearrange("p (h r) -> p h r", h=HG),
                                AX.X, ALU.max, negate=True).then_inc(s_ff[(6 + k) % 2], 1)
                if k == NT * NG - 1:
                    dve.wait_ge(s_ff[0], (NFU // 2) * m + 11)
                    dve.wait_ge(s_ff[1], (NFU // 2) * m + 11)

            def front_max_parts(m):
                link(v.tensor_copy(NMP[:, :, 0, :], NM[:, :, :]))
                link(v.tensor_tensor(NMR[:, :, :], NM[:, :, :], NMP[:, :, 0, :], ALU.subtract))
                link(v.tensor_copy(NMP[:, :, 1, :], NMR[:, :, :]))
                v.tensor_tensor(NMP[:, :, 2, :], NMR[:, :, :], NMP[:, :, 1, :], ALU.subtract).then_inc(s_nm, 1)

            def hand_over(m):
                dve.wait_ge(s_ur, NJ * m)
                v.tensor_copy(xh[:, :], xh_f[:, :].bitcast(f32))
                v.tensor_copy(xl[:, :], xl_f[:, :].bitcast(f32)).then_inc(s_xb, 1)

            def hidden(n, j):
                dve.wait_ge(s_tg, NJ * n + j + 1)
                v.scalar_tensor_tensor(out=H0[:, :], in0=TG[:, j % 2, :], scalar=1.0, in1=pG[:, :],
                                       op0=ALU.add, op1=ALU.mult).then_inc(s_h0, 1)
                dve.wait_ge(s_h0, NJ * n + j + 1)
                dve.wait_ge(s_ur, NJ * n + j + 1)
                dve.wait_ge(s_dn, NJ * n + max(j - 1, 0))
                if j < SH:
                    v.tensor_tensor(H1[:, :], pU[:, :], H0[:, :], ALU.mult).then_inc(s_h1, 1)
                    dve.wait_ge(s_h1, NJ * n + j + 1)
                    dve.wait_ge(s_cr, SH * n + j + 1)
                    v.scalar_tensor_tensor(out=HID[:, j % 2, :], in0=pC[:, :], scalar=0.5, in1=H1[:, :],
                                           op0=ALU.mult, op1=ALU.mult).then_inc(s_hid, 1)
                else:
                    v.scalar_tensor_tensor(out=HID[:, j % 2, :], in0=pU[:, :], scalar=0.5, in1=H0[:, :],
                                           op0=ALU.mult, op1=ALU.mult).then_inc(s_hid, 1)
                    dve.wait_ge(s_hid, NJ * n + j + 1)
                    dve.sem_inc(s_h1, 1)

            def invert(n):
                dve.wait_ge(s_dc, 16 * n + 16)
                dve.wait_ge(s_rd, 16 * n)
                v.reciprocal(RC[:, :], DC[:, :]).then_inc(s_rc, 1)

            def finish(n):
                dve.wait_ge(s_fT, n + 1)
                dve.wait_ge(s_xr, 16 * n + 16)
                dve.wait_ge(s_os, 16 * n)
                v.tensor_tensor(OS[:, :, :].rearrange("p t c -> p (t c)"), pS[:, :],
                                XR[:, :, :].rearrange("p t c -> p (t c)"), ALU.add).then_inc(s_fa, 1)

            def iteration(n, ahead):
                m = n + 1
                for j in range(NJ):
                    if ahead and j == 1:
                        front_norm(m)
                    hidden(n, j)
                    if ahead:
                        if j == 1:
                            front_split(m)
                        elif j in (2, 3):
                            front_qk(m, j - 2)
                        elif j == 9:
                            front_route_a(m)
                        elif j == 11:
                            front_route_b(m)
                        elif j == 13:
                            front_route_c(m)
                        if j >= 9:
                            for k in range((j - 9) * 2, (j - 9) * 2 + 2):
                                front_max(m, k)
                    if j == 12:
                        invert(n)
                if ahead:
                    front_max_parts(m)
                    hand_over(m)
                finish(n)

            front_norm(0)
            front_split(0)
            front_qk(0, 0)
            front_qk(0, 1)
            front_route_a(0)
            front_route_b(0)
            front_route_c(0)
            for k in range(NT * NG):
                front_max(0, k)
            front_max_parts(0)
            hand_over(0)
            before = chain["k"]
            LINKS = 32
            iteration(0, True)
            assert chain["k"] == before + LINKS, chain
            with dve.Fori(1, NBLK - 1) as n:
                chain["base"], chain["k"] = n * LINKS + before, 0
                iteration(n, True)
                assert chain["k"] == LINKS, chain
            chain["base"], chain["k"] = before + LINKS * (NBLK - 1), 0
            iteration(NBLK - 1, False)


_INS = ["L0_attn_x", "L0_attn_Wq", "L0_attn_Wk", "L0_attn_Wv", "L0_attn_Wo", "L0_attn_last_k_init",
        "L0_attn_last_v_init", "L0_ffn_gate_w", "L0_ffn_gate_bias", "L0_ffn_w_gate", "L0_ffn_w_up",
        "L0_ffn_w_down", "L0_ffn_sh_gate", "L0_ffn_sh_up", "L0_ffn_sh_down"]


def kernel(**inputs):
    import numpy as _np
    import concourse.bacc as _bacc
    from concourse import mybir as _mybir
    from concourse.bass_utils import run_bass_kernel_spmd as _run

    nc = _bacc.Bacc("TRN2", target_bir_lowering=False, num_devices=1)
    arrays, args = {}, []
    for name in _INS:
        a = _np.ascontiguousarray(inputs[name])
        arrays[name + "_dram"] = a
        args.append(nc.dram_tensor(name + "_dram", a.shape, _mybir.dt.from_np(a.dtype), kind="ExternalInput").ap())
    shape = inputs["L0_attn_x"].shape
    args.append(nc.dram_tensor("out_dram", shape, _mybir.dt.float32, kind="ExternalOutput").ap())
    attention_and_experts(nc, *args)
    r = _run(nc, [arrays], core_ids=[0])
    return r.results[0]["out_dram"]
```

```python
from contextlib import ExitStack

import concourse.bass as bass
from concourse import mybir


def attention_and_experts(nc: bass.Bass, x, wq, wk, wv, wo, k_init, v_init, gate_w, gate_bias,
                          w_gate, w_up, w_down, sh_gate, sh_up, sh_down, out):
    f32, f32r, bf16 = mybir.dt.float32, mybir.dt.float32r, mybir.dt.bfloat16
    ALU, ACT, AX = mybir.AluOpType, mybir.ActivationFunctionType, mybir.AxisListType

    P = 128
    NSEQ, L, D = x.shape
    TB = 512
    NBLK = NSEQ * L // TB
    NT = TB // P
    SEQ = TB // L
    WIN = k_init.shape[0] + 1
    H, DH = k_init.shape[1:]
    HG = 4
    NG = H // HG
    NQ = L // WIN
    E, I, _ = w_gate.shape
    TOPK, NGRP, TKG, ROUTE_SCALE = 8, 8, 4, 2.5
    NJ = E * I // P + 1
    SH = NJ - 1
    SCALE = float(DH) ** -0.5
    NEG = -3.0e38
    TAKEN = -3.0e38
    PAIRS = [(0, 3), (3, 5), (5, 6)]
    NR = 6
    M_ROW = NR * DH
    MASK_ROW = 64

    x_t = x.rearrange("(n s) (c p) d -> n p (s c) d", s=SEQ, p=P)
    out_t = out.rearrange("(n s) (c p) d -> n p (s c) d", s=SEQ, p=P)

    ctx = ExitStack()
    with ctx:
        def sb(name, shape, dt=f32):
            return ctx.enter_context(nc.sbuf_tensor(name, shape, dt))

        def sem(name):
            return ctx.enter_context(nc.semaphore(name))

        def dram(name, shape, dt):
            return nc.dram_tensor(name, shape, dt, kind="Internal").ap()

        q_dram = dram("q_dram", [P, NR, TB], bf16)
        k_dram = [dram(f"k{s}_dram", [P, NR, WIN + L], bf16) for s in range(SEQ)]
        m_dram = dram("m_dram", [3 * H, TB], bf16)
        zero_dram = dram("zero_dram", [3, H * TB], bf16)

        ident = sb("ident", [P, P])
        identb = sb("identb", [P, P], bf16)
        ones_h = sb("ones_h", [P, HG, 32])
        maskb = sb("maskb", [P, P], bf16)
        sel = sb("sel", [3 * E, SH, P], bf16)
        bias = sb("bias", [P, E])
        half_neg = sb("half_neg", [P, NT])
        whi = sb("whi", [P, 3 * NJ + 2, P], f32r)
        wlo = sb("wlo", [P, 3 * NJ + 2, P], f32r)
        wf = sb("wf", [P, 3, P])
        WQ, WK, GATE = 0, 1, 2
        UP, DOWN = GATE + NJ, GATE + 2 * NJ
        WV, WO, WR = 0, 1, 2

        X = sb("X", [P, NT, P])
        XN = sb("XN", [P, NT, P])
        xnT = sb("xnT", [P, TB])
        xh_f = sb("xh_f", [P, TB], f32r)
        xl_f = sb("xl_f", [P, TB], f32r)
        stats = sb("stats", [P, NT, 6])
        mv = sb("mv", [P, NT, 2])
        veps = sb("veps", [P, NT])
        rstd = sb("rstd", [P, NT])
        QKF = sb("QKF", [P, 2, TB])
        QP = sb("QP", [P, 3, TB], bf16)
        KP = sb("KP", [P, 3, TB], bf16)
        V_STEP = P + DH
        V = sb("V", [P, SEQ * NQ, HG * V_STEP])
        QS = sb("QS", [P, H, TB], bf16)
        KS = sb("KS", [P, 2, H, SEQ, 2 * P], bf16)
        NM = sb("NM", [P, NT, H])
        NMR = sb("NMR", [P, NT, H])
        NMP = sb("NMP", [P, NT, 3, H], bf16)
        MT = sb("MT", [3 * H, TB], bf16)
        ki = sb("ki", [P, WIN])
        kir = sb("kir", [P, WIN])
        kip = sb("kip", [P, 3, WIN], bf16)
        SC = sb("SC", [P, NT, E])
        SB_ = sb("SB_", [P, NT, E])
        pmax = sb("pmax", [P, NT * NGRP, 2])
        pmin = sb("pmin", [P, NT * NGRP, 2])
        g1 = sb("g1", [P, NT * NGRP])
        g2 = sb("g2", [P, NT * NGRP])
        g3 = sb("g3", [P, NT * NGRP])
        GS = sb("GS", [P, NT, NGRP + 4])
        GR = sb("GR", [P, NT, NGRP + 4])
        top = sb("top", [P, NT, 8])
        MS = sb("MS", [P, NT, E])
        MR = sb("MR", [P, NT, E])
        den4 = sb("den4", [P, NT])
        CW = sb("CW", [P, NT, E])
        CP = sb("CP", [P, NT, 3, E], bf16)
        CS = sb("CS", [3 * E, TB], bf16)
        xh = sb("xh", [P, TB], f32r)
        xl = sb("xl", [P, TB], f32r)
        SG = sb("SG", [P, 2, TB])
        HID = sb("HID", [P, 2, TB])
        HH = sb("HH", [P, 4, TB], f32r)
        HL = sb("HL", [P, 4, TB], f32r)
        PT = sb("PT", [P, 4, TB])
        RD = sb("RD", [P, L])
        O = sb("O", [P, TB])
        OT = sb("OT", [P, TB])
        XR = sb("XR", [P, NT, P])

        def bank(name):
            return ctx.enter_context(nc.psum_tensor(name, [P, 512], f32))

        pG, pU, pC, pO, pS, pV = (bank(n) for n in ("pG", "pU", "pC", "pO", "pS", "pV"))
        pF = [bank("pF0"), bank("pF1")]

        stage = KS[:, :, :, :, :].rearrange("p a h s c -> p (a h s c)").bitcast(f32).rearrange("p (j c) -> p j c", c=P)
        J_V = DOWN + NJ
        J_O, J_R, J_KI = J_V + 1, J_V + 2, J_V + 3
        WGROUPS = [(J_V, J_KI), (J_KI, J_KI + 1)] + [(j, min(j + 4, J_V)) for j in range(0, J_V, 4)]
        WBANKS = (pG, pU, pC, pO, pS, pV)
        NWT = len(WGROUPS)

        s_w = sem("small_weights_loaded")
        s_wb = [sem("gate_loaded"), sem("up_loaded"), sem("down_loaded")]
        s_small = sem("small_loaded")
        s_ident = sem("identity_steps")
        s_const = sem("pool_constants")
        s_stage0 = sem("stage_cleared")
        s_wT = sem("weights_transposed")
        s_wh = sem("weights_high_half")
        s_wc = sem("weights_copied")
        s_ki = sem("key_init_split")
        s_kid = sem("key_init_stored")
        s_zero = sem("zero_rows_stored")
        s_clear = sem("query_stack_cleared")
        s_ones = sem("ones_rows_filled")
        s_fill = sem("mask_rows_filled")
        s_identb = sem("identity_bf16_done")
        s_vinit = sem("value_init_loaded")
        s_vz = sem("values_zeroed")

        s_xl = sem("x_loaded")
        s_xn = sem("xn_done")
        s_var = sem("variance_done")
        s_rstd = sem("rstd_done")
        s_xT = sem("xT_copied")
        s_xhl = sem("xT_split")
        s_fr = sem("front_bank_ready")
        s_ff = [sem("front_bank0_free"), sem("front_bank1_free")]
        s_qkf = sem("qk_copied")
        s_p2 = sem("qk_parts12_done")
        s_p3 = sem("qk_part3_done")
        s_pst = sem("qk_parts_stored")
        s_stk = [sem("stacks0_loaded"), sem("stacks1_loaded")]
        s_nm = sem("max_parts_done")
        s_mt = sem("max_rows_copied")
        s_md = sem("max_rows_stored")
        s_mr = sem("max_rows_stacked")
        s_lg = sem("router_logits_copied")
        s_ez = sem("router_exp_done")
        s_cp = sem("combine_parts_done")
        s_cs = sem("combine_rows_copied")
        s_xb = sem("x_handed_over")

        s_gr = sem("gate_ready")
        s_sg = sem("silu_done")
        s_ur = sem("up_ready")
        s_h1 = sem("up_used")
        s_cr = sem("combine_bank_ready")
        s_hid = sem("hidden_ready")
        s_hh = sem("hidden_high_done")
        s_hl = sem("hidden_low_done")
        s_dn = sem("down_done")
        s_st = sem("scores_ready")
        s_ex = sem("exp_done")
        s_pv = sem("pv_done")
        s_on = sem("attention_normalised")
        s_or = sem("outT_ready")
        s_oc = sem("outT_copied")
        s_fT = sem("out_transposed")
        s_fa = sem("residual_added")
        s_xr = sem("residual_loaded")
        s_os = sem("out_stored")
        s_dve = sem("dve_chain")
        s_passed, s_passed_pe, s_passed_dve = (sem(f"waits_passed_{e}") for e in ("sp", "pe", "dve"))

        NFU = 24
        NU = SEQ * NQ
        NS = NU * 2
        J_ATT = 6
        LAG = 3
        ROUTER, VALUES, MAXIMA, CROWS, MROWS = 3, 4, 6, 22, 23
        M0 = 8
        NSTK = 4
        NPST = len(PAIRS) * (1 + SEQ)

        def flat(t):
            return t[:, :, :].rearrange("p t e -> p (t e)")

        def up_bank(j):
            return (pU, pV)[j % 2]

        def combine_bank(j):
            return pS if j % 2 and j != J_ATT - 1 else pC

        block = ctx.enter_context(nc.Block())

        @block.sync
        def _(sp):
            def rows(ap):
                return ap.rearrange("(j p) d -> p j d", p=P)

            sp.dma_start(X[:, :, :], x_t[0]).then_inc(s_xl, 16)
            sp.wait_ge(s_stage0, 1)
            sp.dma_start(stage[:, WQ, :], wq).then_inc(s_w, 16)
            sp.dma_start(stage[:, WK, :], wk).then_inc(s_w, 16)
            sp.dma_start(stage[:, J_V, :], wv).then_inc(s_w, 16)
            sp.dma_start(stage[:, J_O, :], wo).then_inc(s_w, 16)
            sp.dma_start(stage[0:E, J_R, :], gate_w).then_inc(s_w, 16)
            sp.dma_start(stage[1:WIN, J_KI, :], k_init.rearrange("w h d -> w (h d)")).then_inc(s_w, 16)
            sp.dma_start(stage[:, GATE:GATE + SH, :], rows(w_gate.rearrange("e i h -> (e i) h"))).then_inc(s_wb[0], 16)
            sp.dma_start(stage[:, GATE + SH, :], sh_gate).then_inc(s_wb[0], 16)
            sp.dma_start(stage[:, UP:UP + SH, :], rows(w_up.rearrange("e i h -> (e i) h"))).then_inc(s_wb[1], 16)
            sp.dma_start(stage[:, UP + SH, :], sh_up).then_inc(s_wb[1], 16)
            sp.dma_start(stage[:, DOWN:DOWN + SH, :].rearrange("p j (a i) -> p (j a) i", i=I),
                         w_down.rearrange("e h i -> h e i")).then_inc(s_wb[2], 16)
            sp.dma_start(stage[:, DOWN + SH, :], sh_down).then_inc(s_wb[2], 16)
            sp.dma_start(bias[:, :], gate_bias.rearrange("(a e) -> a e", a=1).broadcast_to([P, E])).then_inc(s_small, 16)
            def pairs(dst, parts, repeated):
                if repeated:
                    return [(dst[:, r0:r1, :], parts[:, a:a + 1, :].broadcast_to([P, r1 - r0, parts.shape[2]]))
                            for a, (r0, r1) in enumerate(PAIRS)]
                return [(dst[:, r0:r1, :], parts[:, 0:r1 - r0, :]) for r0, r1 in PAIRS]

            sp.wait_ge(s_clear, 1)
            sp.dma_start(zero_dram, QS[32:35, :, :]).then_inc(s_zero, 16)
            sp.wait_ge(s_ki, 1)
            for s in range(SEQ):
                for dst, src in pairs(k_dram[s][:, :, 0:WIN], kip, True):
                    sp.dma_start(dst, src).then_inc(s_kid, 16)

            def wait(sem, value):
                sp.wait_ge(sem, value)
                if not isinstance(value, int):
                    sp.sem_inc(s_passed, 1)

            def front_parts(m):
                if not isinstance(m, int) or m > 0:
                    for s in range(SEQ):
                        wait(s_stk[s], m * (16 * NSTK))
                wait(s_p3, 2 * m + 1)
                wait(s_p2, 2 * m + 1)
                for dst, src in pairs(q_dram, QP, False):
                    sp.dma_start(dst, src).then_inc(s_pst, 16)
                wait(s_p3, 2 * m + 2)
                wait(s_p2, 2 * m + 2)
                for s in range(SEQ):
                    for dst, src in pairs(k_dram[s][:, :, WIN:WIN + L], KP[:, :, s * L:(s + 1) * L], True):
                        sp.dma_start(dst, src).then_inc(s_pst, 16)

            def stacked(t):
                return t.rearrange("(h d) r t -> (d r) h t", d=DH)

            def query_stack(s):
                own = slice(s * L, (s + 1) * L)
                sp.dma_start(QS[0:M_ROW, :, own], stacked(q_dram)[:, :, own]).then_inc(s_stk[s], 16)
                sp.dma_start(QS[M_ROW:M_ROW + 3, :, own],
                             zero_dram.rearrange("a (h t) -> a h t", h=H)[:, :, own]).then_inc(s_stk[s], 16)

            def key_stacks(s):
                for a in range(2):
                    sp.dma_start(KS[0:M_ROW, a, :, s, :],
                                 stacked(k_dram[s])[:, :, a * WIN:a * WIN + L]).then_inc(s_stk[s], 16)

            def front_stacks(m):
                wait(s_pst, 16 * NPST * m + 16 * NPST)
                for s in range(SEQ):
                    wait(s_st, NS * m - NS // SEQ * (SEQ - 1 - s))
                    query_stack(s)
                    key_stacks(s)

            def max_rows(m):
                wait(s_mt, m + 1)
                sp.dma_start(m_dram, MT[:, :]).then_inc(s_md, 16)
                wait(s_md, 16 * m + 16)
                sp.dma_start(QS[M_ROW:M_ROW + 3, :, :],
                             m_dram.rearrange("(a h) t -> a h t", a=3)).then_inc(s_mr, 16)

            def store(n):
                wait(s_fa, n + 1)
                sp.dma_start(out_t[n], XR[:, :, :]).then_inc(s_os, 16)

            def load_x(m):
                wait(s_xn, m)
                sp.dma_start(X[:, :, :], x_t[m]).then_inc(s_xl, 16)

            def iteration(n, ahead, load):
                max_rows(n)
                if not isinstance(n, int) or n > 0:
                    store(n - 1)
                    wait(s_os, 16 * n)
                sp.dma_start(XR[:, :, :], x_t[n]).then_inc(s_xr, 16)
                if load:
                    load_x(n + 2)
                if ahead:
                    front_parts(n + 1)
                    front_stacks(n + 1)

            load_x(1)
            front_parts(0)
            sp.wait_ge(s_pst, 16 * NPST)
            sp.wait_ge(s_zero, 16)
            for s in range(SEQ):
                query_stack(s)
            sp.wait_ge(s_wc, NWT)
            sp.wait_ge(s_ones, 2)
            sp.wait_ge(s_kid, 16 * len(PAIRS) * SEQ)
            for s in range(SEQ):
                key_stacks(s)
            sp.wait_ge(s_vz, 1)
            for s in range(SEQ):
                for i in range(HG):
                    sp.dma_start(V[1:WIN, s * NQ, i * V_STEP:i * V_STEP + P]
                                 .rearrange("p (g y) -> p g y", y=HG * DH)[:, :, 0:DH],
                                 v_init.rearrange("w (g i) d -> i w g d", i=HG)[i]).then_inc(s_vinit, 16)
            iteration(0, True, True)
            with sp.Fori(1, NBLK - 2) as n:
                iteration(n, True, True)
            iteration(NBLK - 2, True, False)
            iteration(NBLK - 1, False, False)
            store(NBLK - 1)
            sp.wait_ge(s_os, 16 * NBLK)

        @block.gpsimd
        def _(pool):
            def front_rstd(m):
                pool.wait_ge(s_var, m + 1)
                pool.tensor_tensor(rstd[:, :], veps[:, :], half_neg[:, :], ALU.pow).then_inc(s_rstd, 1)

            def front_part3(m, i):
                parts = (QP, KP)[i]
                pool.wait_ge(s_p2, 2 * m + i + 1)
                pool.tensor_tensor(parts[:, 2, :], QKF[:, i, :], parts[:, 1, :], ALU.subtract).then_inc(s_p3, 1)

            pool.memset(half_neg[:, :], -0.5).then_inc(s_const, 1)
            pool.memset(ident[:, :], 0.0).then_inc(s_ident, 1)
            pool.wait_ge(s_ident, 1)
            pool.affine_select(out=ident[:, :], in_=ident[:, :], compare_op=ALU.not_equal, fill=1.0,
                               base=0, pattern=[[-1, P]], channel_multiplier=1).then_inc(s_ident, 1)
            pool.wait_ge(s_const, 1)
            front_rstd(0)
            pool.memset(maskb[:, :], 0.0).then_inc(s_const, 1)
            pool.memset(sel[:, :, :], 0.0).then_inc(s_const, 1)
            pool.memset(ones_h[:, :, :], 0.0).then_inc(s_const, 1)
            pool.wait_ge(s_const, 4)
            pool.affine_select(out=maskb[:, :], in_=maskb[:, :], compare_op=ALU.is_ge, fill=NEG,
                               base=WIN - 1, pattern=[[1, P]], channel_multiplier=-1).then_inc(s_const, 1)
            pool.wait_ge(s_const, 5)
            pool.affine_select(out=maskb[:, :], in_=maskb[:, :], compare_op=ALU.is_ge, fill=NEG,
                               base=0, pattern=[[-1, P]], channel_multiplier=1).then_inc(s_const, 1)
            pool.wait_ge(s_const, 6)
            pool.memset(maskb[32:MASK_ROW, :], 1.0).then_inc(s_const, 1)
            pool.wait_ge(s_const, 7)
            front_part3(0, 0)
            front_part3(0, 1)
            pool.memset(V[:, :, :], 0.0).then_inc(s_vz, 1)
            for a in range(3):
                pool.wait_ge(s_const, 7 + a)
                part = sel[:, :, :].rearrange("p j (b i) -> p j b i", b=2)
                pool.affine_select(out=part, in_=part, compare_op=ALU.not_equal, fill=1.0, base=-E * a,
                                   pattern=[[-2, SH], [-1, 2], [0, I]], channel_multiplier=1).then_inc(s_const, 1)
            for i in range(HG):
                pool.memset(ones_h[:, i, i * DH:(i + 1) * DH], 1.0).then_inc(s_const, 1)

            def low(n, j):
                pool.wait_ge(s_hh, NJ * n + j + 1)
                pool.tensor_tensor(HL[:, j % 4, :], HID[:, j % 2, :], HH[:, j % 4, :].bitcast(f32),
                                   ALU.subtract).then_inc(s_hl, 1)

            def iteration(n, ahead):
                for j in range(NJ):
                    if ahead and j == 1:
                        front_rstd(n + 1)
                    low(n, j)
                    if ahead and j in (5, 6):
                        front_part3(n + 1, j - 5)

            iteration(0, True)
            with pool.Fori(1, NBLK - 1) as n:
                iteration(n, True)
            iteration(NBLK - 1, False)

        @block.tensor
        def _(pe):
            def split3(dst, w, hi, lo):
                nc.tensor.matmul(dst, whi[:, w, :], hi, start=True, stop=False)
                nc.tensor.matmul(dst, whi[:, w, :], lo, start=False, stop=False)
                return nc.tensor.matmul(dst, wlo[:, w, :], hi, start=False, stop=True)

            def use(m, u):
                pe.wait_ge(s_ff[u % 2], m * (NFU // 2) + u // 2)
                return pF[u % 2]

            def front_x(m):
                b = use(m, 0)
                pe.wait_ge(s_xn, m + 1)
                for t in range(NT):
                    last = nc.tensor.transpose(b[:, t * P:(t + 1) * P], XN[:, t, :], ident[:, :])
                last.then_inc(s_fr, 1)

            def front_qk(m):
                pe.wait_ge(s_xhl, m + 1)
                for i, w in enumerate((WQ, WK)):
                    b = use(m, 1 + i)
                    split3(b[:, :], w, xh_f[:, :], xl_f[:, :]).then_inc(s_fr, 1)

            def front_v(m, s):
                b = use(m, VALUES + s)
                t0 = s * L
                nc.tensor.matmul(b[WIN:P, 0:P], xnT[:, t0:t0 + WIN], wf[:, WV, :], start=True, stop=True)
                for w in range(1, NQ):
                    t = t0 + (w - 1) * WIN
                    last = nc.tensor.matmul(b[:, w * P:(w + 1) * P], xnT[:, t:t + P], wf[:, WV, :],
                                            start=True, stop=True)
                last.then_inc(s_fr, 1)

            def front_router(m):
                b = use(m, ROUTER)
                for t in range(NT):
                    last = nc.tensor.matmul(b[:, t * E:(t + 1) * E], xnT[:, t * P:(t + 1) * P],
                                            wf[:, WR, 0:E], start=True, stop=True)
                last.then_inc(s_fr, 1)

            def front_scores(m, k):
                b = use(m, MAXIMA + k)
                t, hg = divmod(k, NG)
                s, c = divmod(t, L // P)
                if k % (NT * NG // SEQ) == 0:
                    pe.wait_ge(s_stk[s], (m + 1) * (16 * NSTK))
                for i in range(HG):
                    h = hg * HG + i
                    for half in range(2):
                        q0 = t * P + half * WIN
                        last = nc.tensor.matmul(b[half * WIN:(half + 1) * WIN, i * P:(i + 1) * P],
                                                QS[:, h, q0:q0 + WIN], KS[:, half, h, s, c * P:(c + 1) * P],
                                                start=True, stop=True)
                last.then_inc(s_fr, 1)

            def front_max(m):
                b = use(m, MROWS)
                pe.wait_ge(s_nm, m + 1)
                pe.sem_inc(s_passed_pe, 1)
                bb = b[:, :].bitcast(bf16)
                for t in range(NT):
                    last = nc.tensor.transpose(bb[0:3 * H, t * P:(t + 1) * P],
                                               NMP[:, t, :, :].rearrange("p a h -> p (a h)"), identb[:, :])
                last.then_inc(s_fr, 1)

            def front_combine(m):
                b = use(m, CROWS)
                pe.wait_ge(s_cp, m + 1)
                bb = b[:, :].bitcast(bf16)
                for t in range(NT):
                    last = nc.tensor.transpose(bb[0:3 * E, t * P:(t + 1) * P],
                                               CP[:, t, :, :].rearrange("p a e -> p (a e)"), identb[:, :])
                last.then_inc(s_fr, 1)

            def gate(n, j):
                if j == 0:
                    pe.wait_ge(s_xb, 2 * (n + 1))
                if j == J_ATT + 1:
                    pe.wait_ge(s_ex, NS * (n + 1))
                pe.wait_ge(s_sg, NJ * n + j)
                split3(pG[:, :], GATE + j, xh[:, :], xl[:, :]).then_inc(s_gr, 1)

            def up(n, j):
                if j in (J_ATT + 1, J_ATT + 2):
                    pe.wait_ge(s_on, SEQ * n + j - J_ATT)
                pe.wait_ge(s_h1, NJ * n + max(j - 1, 0))
                split3(up_bank(j)[:, :], UP + j, xh[:, :], xl[:, :]).then_inc(s_ur, 1)
                if j < SH:
                    if j == 0:
                        pe.wait_ge(s_cs, n + 1)
                    pe.wait_ge(s_hid, NJ * n + (j if j in (J_ATT - 1, J_ATT) else max(j - 1, 0)))
                    nc.tensor.matmul(combine_bank(j)[:, :], sel[:, j, :], CS[:, :],
                                     start=True, stop=True).then_inc(s_cr, 1)

            def down(n, j):
                if j == 0:
                    pe.wait_ge(s_oc, n)
                pe.wait_ge(s_hl, NJ * n + j + 1)
                hh, hl = HH[:, j % 4, :], HL[:, j % 4, :]
                nc.tensor.matmul(pO[:, :], whi[:, DOWN + j, :], hh, start=j == 0, stop=False)
                nc.tensor.matmul(pO[:, :], whi[:, DOWN + j, :], hl, start=False, stop=False)
                last = nc.tensor.matmul(pO[:, :], wlo[:, DOWN + j, :], hh, start=False, stop=j == SH)
                last.then_inc(s_dn, 1)

            def scores(n, k):
                u, half = divmod(k, 2)
                s, w = divmod(u, NQ)
                if k == 0:
                    pe.wait_ge(s_mr, 16 * n + 16)
                    pe.wait_ge(s_hid, NJ * n + 4)
                    pe.wait_ge(s_fa, n)
                elif k == 1:
                    pe.wait_ge(s_sg, NJ * n + J_ATT + 1)
                else:
                    pe.wait_ge(s_ex, NS * n + k - 1)
                q0 = s * L + w * WIN
                for i in range(8):
                    h = half * 8 + i
                    last = nc.tensor.matmul((pS, pG)[half][:, i * WIN:(i + 1) * WIN],
                                            KS[:, w % 2, h, s, (w // 2) * P:(w // 2 + 1) * P],
                                            QS[:, h, q0:q0 + WIN], start=True, stop=True)
                last.then_inc(s_st, 1)

            def weigh(n, u):
                s, w = divmod(u, NQ)
                if w == 0:
                    pe.wait_ge(s_h1, NJ * n + J_ATT + s)
                pe.wait_ge(s_ex, NS * n + 2 * u + 2)
                b = up_bank(J_ATT + 1 - s)
                for c in range(2):
                    cols = slice(c * L + w * WIN, c * L + (w + 1) * WIN)
                    for i in range(HG):
                        for g in range(NG):
                            h = g * HG + i
                            p = PT[:, (2 * u + h // 8) % 4, (h % 8) * WIN:(h % 8 + 1) * WIN]
                            v0 = i * P + g * HG * DH
                            w_t = ones_h[:, i, :] if c else V[:, u, v0:v0 + HG * DH]
                            last = nc.tensor.matmul(b[32 * g:32 * g + 32, cols], w_t, p,
                                                    start=i == 0, stop=i == HG - 1)
                last.then_inc(s_pv, 1)

            def project_out(n):
                pe.wait_ge(s_on, SEQ * (n + 1))
                nc.tensor.matmul(pO[:, :], wf[:, WO, :], O[:, :], start=False, stop=False).then_inc(s_or, 1)

            def finish(n):
                pe.wait_ge(s_oc, n + 1)
                if not isinstance(n, int) or n < NBLK - 1:
                    pe.wait_ge(s_hid, NJ * (n + 1) + 4)
                for t in range(NT):
                    last = nc.tensor.transpose(pS[:, t * P:(t + 1) * P], OT[:, t * P:(t + 1) * P], ident[:, :])
                last.then_inc(s_fT, 1)

            def iteration(n, ahead):
                m = n + 1
                for j in range(NJ):
                    gate(n, j)
                    if j in (0, 1) and (not isinstance(n, int) or n > 0):
                        down(n - 1, SH - 1 + j)
                    if LAG <= j <= J_ATT or j >= J_ATT + LAG:
                        down(n, j - LAG)
                    up(n, j)
                    if j == 1:
                        front_max(n)
                    if j == 4 and (not isinstance(n, int) or n > 0):
                        finish(n - 1)
                    if j == J_ATT + LAG:
                        project_out(n)
                    if ahead:
                        if j == 3:
                            front_x(m)
                        elif j == 4:
                            front_qk(m)
                        elif j == 5:
                            front_router(m)
                        elif M0 <= j < M0 + 8:
                            front_scores(m, 2 * (j - M0))
                            front_scores(m, 2 * (j - M0) + 1)
                    if j == J_ATT:
                        scores(n, 0)
                        scores(n, 1)
                        down(n, J_ATT - 2)
                        down(n, J_ATT - 1)
                        if ahead:
                            for s in range(SEQ):
                                front_v(m, s)
                        for u in range(NU):
                            if u + 1 < NU:
                                scores(n, 2 * u + 2)
                                scores(n, 2 * u + 3)
                            weigh(n, u)
                down(n, SH - 2)
                if ahead:
                    front_combine(m)

            pe.wait_ge(s_ident, 2)
            front_x(0)
            pe.wait_ge(s_w, 16 * 6)
            for k, (j0, j1) in enumerate(WGROUPS):
                if k == len(WBANKS):
                    pe.wait_ge(s_wc, 3)
                    front_qk(0)
                    front_router(0)
                if k >= len(WBANKS):
                    pe.wait_ge(s_wc, k + 1 - len(WBANKS))
                if k >= 2:
                    for a in range(3):
                        if j1 > GATE + a * NJ:
                            pe.wait_ge(s_wb[a], 32)
                for j in range(j0, j1):
                    last = nc.tensor.transpose(WBANKS[k % len(WBANKS)][:, (j - j0) * P:(j - j0 + 1) * P],
                                               stage[:, j, :], ident[:, :])
                last.then_inc(s_wT, 1)
            pe.wait_ge(s_wc, NWT)
            for s in range(SEQ):
                front_v(0, s)
            pe.wait_ge(s_const, 14)
            pe.wait_ge(s_fill, 3)
            pe.wait_ge(s_vinit, 16 * HG * SEQ)
            for k in range(NT * NG):
                front_scores(0, k)
            front_combine(0)
            iteration(0, True)
            with pe.Fori(1, NBLK - 1) as n:
                iteration(n, True)
            iteration(NBLK - 1, False)
            down(NBLK - 1, SH - 1)
            down(NBLK - 1, SH)
            finish(NBLK - 1)

        @block.scalar
        def _(act):
            copy = ACT.Copy
            def copied(u):
                return s_ff[u % 2]

            def front_x(m):
                act.wait_ge(s_fr, NFU * m + 1)
                nc.scalar.activation(xnT[:, :], pF[0][:, :], copy).then_inc(s_xT, 1)
                act.wait_ge(s_xT, m + 1)
                act.sem_inc(copied(0), 1)

            def front_qk(m):
                for i in range(2):
                    act.wait_ge(s_fr, NFU * m + 2 + i)
                    act.wait_ge(s_p3, 2 * m)
                    nc.scalar.activation(QKF[:, i, :], pF[(1 + i) % 2][:, :], copy,
                                         scale=SCALE if i == 0 else 1.0).then_inc(s_qkf, 1)
                    act.wait_ge(s_qkf, 2 * m + i + 1)
                    act.sem_inc(copied(1 + i), 1)

            def front_v(m):
                act.wait_ge(s_pv, NU * m)
                for s in range(SEQ):
                    act.wait_ge(s_fr, NFU * m + VALUES + s + 1)
                    b = pF[(VALUES + s) % 2]
                    for w in range(NQ):
                        rows = slice(0, P) if w else slice(WIN, P)
                        diag = (V[rows, s * NQ + w, :].rearrange("p (i x) -> p i x", x=V_STEP)[:, :, 0:P]
                                .rearrange("p i (g y) -> p i g y", y=HG * DH)[:, :, :, 0:DH])
                        last = nc.scalar.activation(diag, b[rows, w * P:(w + 1) * P]
                                                    .rearrange("p (g i d) -> p i g d", g=NG, i=HG), copy)
                    last.then_inc(copied(VALUES + s), 1)

            def front_router(m):
                act.wait_ge(s_lg, m + 1)
                nc.scalar.activation(flat(SC), flat(SC), ACT.Exp, scale=-1.0).then_inc(s_ez, 1)

            def front_combine(m):
                act.wait_ge(s_fr, NFU * m + CROWS + 1)
                act.wait_ge(s_cr, SH * m)
                nc.scalar.activation(CS[:, :], pF[CROWS % 2][0:3 * E, :].bitcast(bf16)[:, 0:TB], copy).then_inc(s_cs, 1)
                act.wait_ge(s_cs, m + 1)
                act.sem_inc(copied(CROWS), 1)

            def front_max(m):
                act.wait_ge(s_fr, NFU * m + MROWS + 1)
                act.wait_ge(s_md, 16 * m)
                nc.scalar.activation(MT[:, :], pF[MROWS % 2][0:3 * H, :].bitcast(bf16)[:, 0:TB], copy).then_inc(s_mt, 1)
                act.wait_ge(s_mt, m + 1)
                act.sem_inc(copied(MROWS), 1)

            def out_copy(n):
                act.wait_ge(s_dn, NJ * (n + 1))
                act.wait_ge(s_fT, n)
                nc.scalar.activation(OT[:, :], pO[:, :], copy).then_inc(s_oc, 1)

            def hand_over(m):
                act.wait_ge(s_ur, NJ * m)
                act.wait_ge(s_xhl, m + 1)
                nc.scalar.activation(xh[:, :], xh_f[:, :].bitcast(f32), copy).then_inc(s_xb, 1)

            def gate(n, j):
                act.wait_ge(s_gr, NJ * n + j + 1)
                act.wait_ge(s_h1, NJ * n + max(j - 1, 0))
                nc.scalar.activation(SG[:, j % 2, :], pG[:, :], ACT.Silu).then_inc(s_sg, 1)

            def high(n, j):
                act.wait_ge(s_hid, NJ * n + j + 1)
                act.wait_ge(s_dn, NJ * n + max(j - 3, 0))
                nc.scalar.activation(HH[:, j % 4, :], HID[:, j % 2, :], copy).then_inc(s_hh, 1)

            def exps(n, k):
                act.wait_ge(s_st, NS * n + k + 1)
                act.wait_ge(s_pv, NU * n + max(k // 2 - 1, 0))
                nc.scalar.activation(PT[:, k % 4, :], (pS, pG)[k % 2][:, :], ACT.Exp).then_inc(s_ex, 1)

            def iteration(n, ahead):
                m = n + 1
                for j in range(NJ):
                    gate(n, j)
                    if j == 1 and (not isinstance(n, int) or n > 0):
                        out_copy(n - 1)
                    if j >= 1 and j != J_ATT + 1:
                        high(n, j - 1)
                    if j == 1:
                        front_max(n)
                    if ahead:
                        if j == 3:
                            front_x(m)
                        elif j == 4:
                            front_qk(m)
                        elif j == J_ATT + 1:
                            front_v(m)
                    if j == J_ATT:
                        if ahead:
                            front_router(m)
                        for k in range(NS):
                            exps(n, k)
                            if k == 1:
                                high(n, j)
                if ahead:
                    hand_over(m)
                    front_combine(m)
                high(n, SH)

            front_x(0)
            for k, (j0, j1) in enumerate(WGROUPS):
                whole = WBANKS[k % len(WBANKS)]
                act.wait_ge(s_wT, k + 1)
                if k == 0:
                    nc.scalar.activation(wf[:, :, :].rearrange("p j c -> p (j c)"), whole[:, 0:3 * P],
                                         copy).then_inc(s_wc, 1)
                elif k == 1:
                    act.wait_ge(s_wc, 1)
                    nc.scalar.activation(ki[:, :], whole[:, 0:WIN], copy).then_inc(s_wc, 1)
                else:
                    nc.scalar.activation(whi[:, j0:j1, :].rearrange("p j c -> p (j c)"), whole[:, 0:(j1 - j0) * P],
                                         copy).then_inc(s_wh, 1)
                if k == len(WBANKS) - 1:
                    front_qk(0)
                    front_router(0)
            act.wait_ge(s_const, 6)
            act.wait_ge(s_wc, NWT)
            nc.scalar.activation(KS[MASK_ROW:P, 1, :, :, :].rearrange("p h s (c r) -> p (h s c) r", r=P),
                                 maskb[MASK_ROW:P, :].rearrange("p (a r) -> p a r", a=1)
                                 .broadcast_to([P - MASK_ROW, H * SEQ * 2, P]), copy).then_inc(s_fill, 1)
            act.wait_ge(s_vz, 1)
            front_v(0)
            hand_over(0)
            front_combine(0)
            iteration(0, True)
            with act.Fori(1, NBLK - 1) as n:
                iteration(n, True)
            iteration(NBLK - 1, False)
            out_copy(NBLK - 1)

        @block.vector
        def _(dve):
            v = nc.vector
            chain = {"base": 0, "k": 0}

            def link_apart(ins):
                chain["k"] += 1
                ins.then_inc(s_dve, 1)
                dve.wait_ge(s_dve, chain["base"] + chain["k"])
                dve.sem_inc(s_passed_dve, 1)

            def link(ins):
                chain["k"] += 1
                ins.then_inc(s_dve, 1)
                dve.wait_ge(s_dve, chain["base"] + chain["k"])

            def front_stats(m):
                dve.wait_ge(s_xl, 16 * m + 16)
                for t in range(NT):
                    last = v.bn_stats(stats[:, t, :], X[:, t, :])
                link_apart(last)

            def front_variance(m):
                for t in range(NT):
                    last = v.bn_aggr(mv[:, t, :], stats[:, t, :])
                link(last)
                v.tensor_scalar(veps[:, :], mv[:, :, 1], 1e-5, None, ALU.add).then_inc(s_var, 1)

            def front_norm(m):
                dve.wait_ge(s_rstd, m + 1)
                if not isinstance(m, int) or m > 0:
                    dve.wait_ge(s_fr, NFU * (m - 1) + 1)
                for t in range(NT):
                    last = v.tensor_scalar(XN[:, t, :], X[:, t, :], mv[:, t, 0:1], rstd[:, t:t + 1],
                                           ALU.subtract, ALU.mult)
                last.then_inc(s_xn, 1)

            def front_split(m):
                dve.wait_ge(s_xT, m + 1)
                link(v.tensor_copy(xh_f[:, :], xnT[:, :]))
                v.tensor_tensor(xl_f[:, :], xnT[:, :], xh_f[:, :].bitcast(f32), ALU.subtract).then_inc(s_xhl, 1)

            def front_qk(m, i):
                parts = (QP, KP)[i]
                dve.wait_ge(s_qkf, 2 * m + i + 1)
                dve.wait_ge(s_pst, 16 * NPST * m)
                link(v.tensor_copy(parts[:, 0, :], QKF[:, i, :]))
                link(v.tensor_tensor(QKF[:, i, :], QKF[:, i, :], parts[:, 0, :], ALU.subtract))
                v.tensor_copy(parts[:, 1, :], QKF[:, i, :]).then_inc(s_p2, 1)

            def front_logits(m):
                dve.wait_ge(s_fr, NFU * m + ROUTER + 1)
                v.tensor_copy(flat(SC), pF[ROUTER % 2][:, 0:NT * E]).then_inc(s_lg, 1)
                dve.wait_ge(s_lg, m + 1)
                dve.sem_inc(s_ff[ROUTER % 2], 1)

            def front_route_a(m):
                dve.wait_ge(s_ez, m + 1)
                link(v.tensor_scalar(flat(MR), flat(SC), 1.0, None, ALU.add))
                link(v.reciprocal(flat(SC), flat(MR)))
                link(v.tensor_tensor(SB_[:, :, :], SC[:, :, :],
                                     bias[:, :].rearrange("p (a e) -> p a e", a=1).broadcast_to([P, NT, E]), ALU.add))
                pairs = flat(SB_).rearrange("p (g a b) -> p g a b", a=2, b=2)
                v.tensor_tensor(pmax[:, :, :], pairs[:, :, :, 0], pairs[:, :, :, 1], ALU.max)
                link(v.tensor_tensor(pmin[:, :, :], pairs[:, :, :, 0], pairs[:, :, :, 1], ALU.min))
                v.tensor_tensor(g1[:, :], pmax[:, :, 0], pmax[:, :, 1], ALU.max)
                v.tensor_tensor(g2[:, :], pmax[:, :, 0], pmax[:, :, 1], ALU.min)
                link(v.tensor_tensor(g3[:, :], pmin[:, :, 0], pmin[:, :, 1], ALU.max))
                link(v.tensor_tensor(g2[:, :], g2[:, :], g3[:, :], ALU.max))
                link_apart(v.tensor_tensor(GS[:, :, 0:NGRP], g1[:, :].rearrange("p (t g) -> p t g", t=NT),
                                     g2[:, :].rearrange("p (t g) -> p t g", t=NT), ALU.add))

            def front_route_b(m):
                for t in range(NT):
                    last = v.max(top[:, t, :], GS[:, t, :])
                link_apart(last)
                for t in range(NT):
                    last = v.match_replace(out=GR[:, t, :], in_to_replace=top[:, t, :], in_values=GS[:, t, :],
                                           imm_value=TAKEN)
                link(last)
                link(v.tensor_scalar(GR[:, :, 0:NGRP], GR[:, :, 0:NGRP], TAKEN, None, ALU.is_equal))
                link(v.tensor_tensor(MS[:, :, :].rearrange("p t (g a) -> p t g a", g=NGRP),
                                     SB_[:, :, :].rearrange("p t (g a) -> p t g a", g=NGRP),
                                     GR[:, :, 0:NGRP].rearrange("p t (g a) -> p t g a", a=1)
                                     .broadcast_to([P, NT, NGRP, E // NGRP]), ALU.mult))
                link(v.tensor_scalar(flat(MS), flat(MS), 0.0, None, ALU.add))

            def front_route_c(m):
                for t in range(NT):
                    last = v.max(top[:, t, :], MS[:, t, :])
                link_apart(last)
                for t in range(NT):
                    last = v.match_replace(out=MR[:, t, :], in_to_replace=top[:, t, :], in_values=MS[:, t, :],
                                           imm_value=TAKEN)
                link(last)
                link(v.scalar_tensor_tensor(out=flat(CW), in0=flat(MR), scalar=TAKEN, in1=flat(SC),
                                            op0=ALU.is_equal, op1=ALU.mult))
                link(v.tensor_reduce(den4[:, :], CW[:, :, :], AX.X, ALU.add))
                link(v.tensor_scalar(den4[:, :], den4[:, :], 1e-20, None, ALU.add))
                link(v.reciprocal(den4[:, :], den4[:, :]))
                for t in range(NT):
                    last = v.tensor_scalar(CW[:, t, :], CW[:, t, :], den4[:, t:t + 1], ROUTE_SCALE, ALU.mult, ALU.mult)
                link(last)
                link(v.tensor_copy(CP[:, :, 0, :], CW[:, :, :]))
                link(v.tensor_tensor(CW[:, :, :], CW[:, :, :], CP[:, :, 0, :], ALU.subtract))
                link(v.tensor_copy(CP[:, :, 1, :], CW[:, :, :]))
                v.tensor_tensor(CP[:, :, 2, :], CW[:, :, :], CP[:, :, 1, :], ALU.subtract).then_inc(s_cp, 1)

            def front_max(m, k):
                t, hg = divmod(k, NG)
                dve.wait_ge(s_fr, NFU * m + MAXIMA + k + 1)
                v.tensor_reduce(NM[:, t, hg * HG:(hg + 1) * HG],
                                pF[(MAXIMA + k) % 2][:, :].rearrange("p (h r) -> p h r", h=HG),
                                AX.X, ALU.max, negate=True).then_inc(s_ff[(MAXIMA + k) % 2], 1)
                if k == NT * NG - 1:
                    dve.wait_ge(s_ff[0], (NFU // 2) * m + 11)
                    dve.wait_ge(s_ff[1], (NFU // 2) * m + 11)

            def front_max_parts(m):
                link(v.tensor_copy(NMP[:, :, 0, :], NM[:, :, :]))
                link(v.tensor_tensor(NMR[:, :, :], NM[:, :, :], NMP[:, :, 0, :], ALU.subtract))
                link(v.tensor_copy(NMP[:, :, 1, :], NMR[:, :, :]))
                v.tensor_tensor(NMP[:, :, 2, :], NMR[:, :, :], NMP[:, :, 1, :], ALU.subtract).then_inc(s_nm, 1)

            def hand_over(m):
                dve.wait_ge(s_ur, NJ * m)
                v.tensor_copy(xl[:, :], xl_f[:, :].bitcast(f32)).then_inc(s_xb, 1)

            def hidden_up(n, j):
                dve.wait_ge(s_sg, NJ * n + j + 1)
                dve.wait_ge(s_ur, NJ * n + j + 1)
                dve.wait_ge(s_hl, NJ * n + max(j - 1, 0))
                done = s_h1 if j < SH else s_hid
                v.tensor_tensor(HID[:, j % 2, :], up_bank(j)[:, :], SG[:, j % 2, :], ALU.mult).then_inc(done, 1)
                if j == SH:
                    dve.wait_ge(s_hid, NJ * n + j + 1)
                    dve.sem_inc(s_h1, 1)

            def hidden_weighted(n, j):
                dve.wait_ge(s_h1, NJ * n + j + 1)
                dve.wait_ge(s_cr, SH * n + j + 1)
                v.tensor_tensor(HID[:, j % 2, :], combine_bank(j)[:, :], HID[:, j % 2, :],
                                ALU.mult).then_inc(s_hid, 1)

            def normalise(n, s):
                dve.wait_ge(s_pv, NU * n + NQ * (s + 1))
                dve.wait_ge(s_or, n)
                if s > 0:
                    dve.wait_ge(s_on, SEQ * n + s)
                b = up_bank(J_ATT + 1 - s)
                link(v.reciprocal(RD[:, :], b[:, L:2 * L]))
                v.tensor_tensor(O[:, s * L:(s + 1) * L], b[:, 0:L], RD[:, :], ALU.mult).then_inc(s_on, 1)

            def finish(n):
                dve.wait_ge(s_fT, n + 1)
                dve.wait_ge(s_xr, 16 * n + 16)
                xr = XR[:, :, :].rearrange("p t c -> p (t c)")
                v.tensor_tensor(xr, pS[:, :], xr, ALU.add).then_inc(s_fa, 1)

            def iteration(n, ahead):
                m = n + 1
                for j in range(NJ):
                    if ahead and j == 0:
                        front_stats(m)
                    if ahead and j == SH:
                        hand_over(m)
                    hidden_up(n, j)
                    k = 2 * (j - M0)
                    if ahead and 0 <= k < NT * NG:
                        front_max(m, k)
                    if j == 5 and (not isinstance(n, int) or n > 0):
                        finish(n - 1)
                    if j < SH:
                        hidden_weighted(n, j)
                    if ahead and 0 <= k < NT * NG:
                        front_max(m, k + 1)
                    if ahead:
                        if j == 0:
                            front_variance(m)
                        elif j == 2:
                            front_norm(m)
                        elif j == 3:
                            front_split(m)
                        elif j == 4:
                            front_qk(m, 0)
                        elif j == 5:
                            front_logits(m)
                            front_qk(m, 1)
                        elif j == J_ATT:
                            front_route_a(m)
                            front_route_b(m)
                    if j == J_ATT:
                        normalise(n, 0)
                        if ahead:
                            front_route_c(m)
                        normalise(n, 1)
                if ahead:
                    front_max_parts(m)

            v.memset(stage[:, J_R:J_KI + 1, :], 0.0).then_inc(s_stage0, 1)
            front_stats(0)
            front_variance(0)
            v.memset(GS[:, :, NGRP:NGRP + 4], 3.0e38)
            dve.wait_ge(s_ident, 2)
            v.tensor_copy(identb[:, :], ident[:, :]).then_inc(s_identb, 1)
            front_norm(0)
            dve.wait_ge(s_identb, 1)
            for r0, then in ((32, s_clear), (MASK_ROW, s_fill)):
                r1 = MASK_ROW if r0 == 32 else P
                v.tensor_copy(QS[r0:r1, :, :].rearrange("p h (c q) -> p (h c) q", q=WIN),
                              identb[r0:r1, MASK_ROW:P].rearrange("p (a q) -> p a q", a=1)
                              .broadcast_to([r1 - r0, H * NT * 2, WIN])).then_inc(then, 1)
            front_split(0)
            dve.wait_ge(s_wc, 2)
            link(v.tensor_copy(kip[:, 0, :], ki[:, :]))
            link(v.tensor_tensor(kir[:, :], ki[:, :], kip[:, 0, :], ALU.subtract))
            link(v.tensor_copy(kip[:, 1, :], kir[:, :]))
            v.tensor_tensor(kip[:, 2, :], kir[:, :], kip[:, 1, :], ALU.subtract).then_inc(s_ki, 1)
            for k in range(2, NWT):
                j0, j1 = WGROUPS[k]
                dve.wait_ge(s_wh, k - 1)
                v.tensor_tensor(wlo[:, j0:j1, :].rearrange("p j c -> p (j c)"),
                                WBANKS[k % len(WBANKS)][:, 0:(j1 - j0) * P],
                                whi[:, j0:j1, :].rearrange("p j c -> p (j c)").bitcast(f32),
                                ALU.subtract).then_inc(s_wc, 1)
                if k == len(WBANKS) - 1:
                    front_qk(0, 0)
                    front_qk(0, 1)
                    front_logits(0)
            dve.wait_ge(s_wc, NWT)
            dve.wait_ge(s_const, 7)
            rows = maskb[32:MASK_ROW, :].rearrange("p (a r) -> p a r", a=1)
            for a in range(2):
                v.tensor_copy(KS[32:MASK_ROW, a, :, :, :].rearrange("p h s (c r) -> p (h s c) r", r=P),
                              rows.broadcast_to([32, H * SEQ * 2, P])).then_inc(s_ones, 1)
            v.tensor_copy(KS[MASK_ROW:P, 0, :, :, :].rearrange("p h s (c r) -> p (h s c) r", r=P),
                          maskb[MASK_ROW:P, :].rearrange("p (a r) -> p a r", a=1)
                          .broadcast_to([P - MASK_ROW, H * SEQ * 2, P])).then_inc(s_fill, 1)
            dve.wait_ge(s_small, 16)
            front_route_a(0)
            front_route_b(0)
            front_route_c(0)
            hand_over(0)
            for k in range(NT * NG):
                front_max(0, k)
            front_max_parts(0)
            before = chain["k"]
            LINKS = 34
            iteration(0, True)
            assert chain["k"] == before + LINKS, chain
            with dve.Fori(1, NBLK - 1) as n:
                chain["base"], chain["k"] = n * LINKS + before, 0
                iteration(n, True)
                assert chain["k"] == LINKS, chain
            chain["base"], chain["k"] = before + LINKS * (NBLK - 1), 0
            iteration(NBLK - 1, False)
            finish(NBLK - 1)


_INS = ["L0_attn_x", "L0_attn_Wq", "L0_attn_Wk", "L0_attn_Wv", "L0_attn_Wo", "L0_attn_last_k_init",
        "L0_attn_last_v_init", "L0_ffn_gate_w", "L0_ffn_gate_bias", "L0_ffn_w_gate", "L0_ffn_w_up",
        "L0_ffn_w_down", "L0_ffn_sh_gate", "L0_ffn_sh_up", "L0_ffn_sh_down"]


def kernel(**inputs):
    import numpy as _np
    import concourse.bacc as _bacc
    from concourse import mybir as _mybir
    from concourse.bass_utils import run_bass_kernel_spmd as _run

    nc = _bacc.Bacc("TRN2", target_bir_lowering=False, num_devices=1)
    arrays, args = {}, []
    for name in _INS:
        a = _np.ascontiguousarray(inputs[name])
        arrays[name + "_dram"] = a
        args.append(nc.dram_tensor(name + "_dram", a.shape, _mybir.dt.from_np(a.dtype), kind="ExternalInput").ap())
    shape = inputs["L0_attn_x"].shape
    args.append(nc.dram_tensor("out_dram", shape, _mybir.dt.float32, kind="ExternalOutput").ap())
    attention_and_experts(nc, *args)
    r = _run(nc, [arrays], core_ids=[0])
    return r.results[0]["out_dram"]
```
